# Optimizing a Trainium2 kernel written in Bass

```python
import numpy as np
import jax
import jax.numpy as jnp

def _softmax(x, axis=-1):
    return jax.nn.softmax(x, axis=axis)

def _gelu(x):
    return jax.nn.gelu(x, approximate=True)

def _silu(x):
    return jax.nn.silu(x)

def _sigmoid(x):
    return jax.nn.sigmoid(x)

def _layernorm(x, axis=-1, eps=1e-05):
    m = jnp.mean(x, axis=axis, keepdims=True)
    v = jnp.var(x, axis=axis, keepdims=True)
    return (x - m) / jnp.sqrt(v + eps)

def _scatter_add(tgt, idx, src, axis=0):
    return tgt.at[idx].add(src)

def _segment_sum(src, seg, n):
    return jax.ops.segment_sum(src, seg, n)
kernel_name = 'mk_xattn_ffn_d1_seqx_r4_bf0003'

def setup_inputs(seed: int=0):
    np.random.seed(seed)
    _w = jnp.asarray

    def _rec_inputs():
        import jax
        import jax.numpy as jnp
        _rk = jax.random.key(seed)
        x = 7.22e-05 + 1 * jax.random.normal(jax.random.fold_in(_rk, 1), (32, 112, 256), jnp.float32)
        _lenS = 112 - jax.random.randint(jax.random.fold_in(_rk, 7), (32,), 0, max(1, 112 // 4) + 1, jnp.int32)
        _lenS2 = 375 - jax.random.randint(jax.random.fold_in(_rk, 8), (32,), 0, max(1, 375 // 4) + 1, jnp.int32)
        _ctx_768P = jax.random.normal(jax.random.fold_in(_rk, 11), (32, 16, 192), jnp.float32)
        _ctx_768c = jax.random.dirichlet(jax.random.fold_in(_rk, 511), 0.3 * jnp.ones((16,), jnp.float32), (32, 375))
        _ctx_768t = jnp.einsum('bsk,bkd->bsd', _ctx_768c, _ctx_768P)
        _ctx_768t = _ctx_768t * jax.lax.rsqrt(jnp.mean(jnp.square(_ctx_768t)) + 1e-12) * 0.953939
        ctx_768 = 2.09791e-05 + 1.00001 * (_ctx_768t + 0.3 * jax.random.normal(jax.random.fold_in(_rk, 611), (32, 375, 192), jnp.float32))
        return (x, ctx_768)
    x, ctx_768 = _rec_inputs()

    def _L0_xattn_setup():
        import jax, jax.numpy as jnp
        import numpy as np
        HEADS = 8
        DIM_HEAD = 64
        SCALE = DIM_HEAD ** (-0.5)
        key = jax.random.key(seed)
        ks = jax.random.split(key, 7)
        b, n, m = (4, 512, 256)
        qd, cd, inner = (256, 192, HEADS * DIM_HEAD)
        s = lambda fan_in: 1.0 / np.sqrt(fan_in)
        return {'x': jax.random.normal(ks[0], (b, n, qd), jnp.float32), 'context': jax.random.normal(ks[1], (b, m, cd), jnp.float32), 'Wq': jax.random.normal(ks[2], (qd, inner), jnp.float32) * s(qd), 'Wk': jax.random.normal(ks[3], (cd, inner), jnp.float32) * s(cd), 'Wv': jax.random.normal(ks[4], (cd, inner), jnp.float32) * s(cd), 'Wout': jax.random.normal(ks[5], (inner, qd), jnp.float32) * s(inner), 'bout': jax.random.normal(ks[6], (qd,), jnp.float32) * 0.01}
    _L0_xattn_all = _L0_xattn_setup()
    _L0_xattn_in = {k: v for k, v in _L0_xattn_all.items() if k in ('Wq', 'Wk', 'Wv', 'Wout', 'bout')}
    del _L0_xattn_all

    def _L0_ffn_setup():
        import jax, jax.numpy as jnp
        import numpy as np
        B, S, D = (2, 512, 256)
        H = 512
        E = 8
        K = 2
        HS = 512 * 1
        SCALE = 1.0 / float(np.sqrt(D))
        key = jax.random.key(seed)
        ks = jax.random.split(key, 9)
        init = 0.02
        return {'x': jax.random.normal(ks[0], (B, S, D), dtype=jnp.float32), 'Wr': jax.random.normal(ks[1], (D, E), dtype=jnp.float32) * init, 'rb': jnp.zeros((E,), dtype=jnp.float32), 'W1': jax.random.normal(ks[2], (E, D, H), dtype=jnp.float32) * init, 'W2': jax.random.normal(ks[3], (E, H, D), dtype=jnp.float32) * init, 'W3': jax.random.normal(ks[4], (E, D, H), dtype=jnp.float32) * init, 'Ws1': jax.random.normal(ks[5], (D, HS), dtype=jnp.float32) * init, 'Ws2': jax.random.normal(ks[6], (HS, D), dtype=jnp.float32) * init, 'Ws3': jax.random.normal(ks[7], (D, HS), dtype=jnp.float32) * init}
    _L0_ffn_all = _L0_ffn_setup()
    _L0_ffn_in = {k: v for k, v in _L0_ffn_all.items() if k in ('Wr', 'rb', 'W1', 'W2', 'W3', 'Ws1', 'Ws2', 'Ws3')}
    del _L0_ffn_all
    return {'x': x, 'ctx_768': ctx_768, 'L0_xattn_Wq': _L0_xattn_in['Wq'], 'L0_xattn_Wk': _L0_xattn_in['Wk'], 'L0_xattn_Wv': _L0_xattn_in['Wv'], 'L0_xattn_Wout': _L0_xattn_in['Wout'], 'L0_xattn_bout': _L0_xattn_in['bout'], 'L0_ffn_Wr': _L0_ffn_in['Wr'], 'L0_ffn_rb': _L0_ffn_in['rb'], 'L0_ffn_W1': _L0_ffn_in['W1'], 'L0_ffn_W2': _L0_ffn_in['W2'], 'L0_ffn_W3': _L0_ffn_in['W3'], 'L0_ffn_Ws1': _L0_ffn_in['Ws1'], 'L0_ffn_Ws2': _L0_ffn_in['Ws2'], 'L0_ffn_Ws3': _L0_ffn_in['Ws3']}

def reference(x, ctx_768, L0_xattn_Wq, L0_xattn_Wk, L0_xattn_Wv, L0_xattn_Wout, L0_xattn_bout, L0_ffn_Wr, L0_ffn_rb, L0_ffn_W1, L0_ffn_W2, L0_ffn_W3, L0_ffn_Ws1, L0_ffn_Ws2, L0_ffn_Ws3):
    import jax
    import jax.numpy as jnp

    def _L0_xattn_ref(x, context, Wq, Wk, Wv, Wout, bout):
        import jax, jax.numpy as jnp
        import numpy as np
        HEADS = 8
        DIM_HEAD = 64
        SCALE = DIM_HEAD ** (-0.5)
        b, n, _ = x.shape
        m = context.shape[1]
        q = (x @ Wq).reshape(b, n, HEADS, DIM_HEAD)
        k = (context @ Wk).reshape(b, m, HEADS, DIM_HEAD)
        v = (context @ Wv).reshape(b, m, HEADS, DIM_HEAD)
        sim = jnp.einsum('bihd,bjhd->bhij', q, k) * SCALE
        attn = jax.nn.softmax(sim, axis=-1)
        out = jnp.einsum('bhij,bjhd->bihd', attn, v).reshape(b, n, HEADS * DIM_HEAD)
        return out @ Wout + bout

    def _L0_ffn_ref(x, Wr, rb, W1, W2, W3, Ws1, Ws2, Ws3):
        import jax, jax.numpy as jnp
        import numpy as np
        B, S, D = (2, 512, 256)
        H = 512
        E = 8
        K = 2
        HS = 512 * 1
        SCALE = 1.0 / float(np.sqrt(D))
        logits = jnp.einsum('bsd,de->bse', x, Wr) * SCALE
        _, idx = jax.lax.top_k(logits + rb, K)
        gathered = jnp.take_along_axis(logits, idx, axis=-1)
        w = jax.nn.softmax(gathered, axis=-1)
        w_full = jnp.sum(jax.nn.one_hot(idx, E, dtype=x.dtype) * w[..., None], axis=-2)
        h = jnp.einsum('bsd,edh->bseh', x, W1) * jax.nn.silu(jnp.einsum('bsd,edh->bseh', x, W3))
        expert_out = jnp.einsum('bseh,ehd->bsed', h, W2)
        out = jnp.einsum('bsed,bse->bsd', expert_out, w_full)
        hs = jnp.einsum('bsd,dh->bsh', x, Ws1) * jax.nn.silu(jnp.einsum('bsd,dh->bsh', x, Ws3))
        out = out + jnp.einsum('bsh,hd->bsd', hs, Ws2)
        return out
    x = x + _L0_xattn_ref(_layernorm(x, axis=-1), ctx_768, L0_xattn_Wq, L0_xattn_Wk, L0_xattn_Wv, L0_xattn_Wout, L0_xattn_bout)
    x = x + _L0_ffn_ref(_layernorm(x, axis=-1), L0_ffn_Wr, L0_ffn_rb, L0_ffn_W1, L0_ffn_W2, L0_ffn_W3, L0_ffn_Ws1, L0_ffn_Ws2, L0_ffn_Ws3)
    return x

_drawn_inputs = setup_inputs


def setup_inputs(seed=0):
    import zlib

    import numpy as np

    out = dict(_drawn_inputs(seed))
    spreads = {'L0_ffn_rb': (0.0, 0.472)}
    factors = {'L0_xattn_bout': 6.182,
     'L0_ffn_Wr': 8.0,
     'L0_ffn_W1': 3.823,
     'L0_ffn_W2': 3.824,
     'L0_ffn_W3': 3.868,
     'L0_ffn_Ws1': 2.677,
     'L0_ffn_Ws3': 2.714}
    for name, (base, spread) in spreads.items():
        noise = np.random.default_rng([zlib.crc32(name.encode()), seed]).standard_normal(out[name].shape)
        drawn = base * np.exp(spread * noise) if base else spread * noise
        out[name] = jnp.asarray(drawn.astype(out[name].dtype))
    for name, factor in factors.items():
        out[name] = (out[name] * factor).astype(out[name].dtype)
    return out
```

```python
from contextlib import ExitStack

import concourse.bass as bass
from concourse import mybir

F32 = mybir.dt.float32
F32R = mybir.dt.float32r
U32 = mybir.dt.uint32
ALU = mybir.AluOpType
ACT = mybir.ActivationFunctionType
AX = mybir.AxisListType

EPS = 1e-5


def wait(eng, sem, count):
    if not isinstance(count, int) or count > 0:
        eng.wait_ge(sem, count)


UNIT_BANKS = 3
PROLOGUE = ["c0", "c1", "k0", "k1", "k2", "k3", "v0", "xt0", "xt1", "v1", "q0", "v2"]
EVEN = [["c0"], ["c1", "q1"], ["k0"], ["k1", "k2"], ["v0"], ["k3", "wout"], ["v1"], ["v2", "xt0", "xt1"]]
ODD = [["c0"], ["c1"], ["k0"], ["k1", "k2"], ["v0"], ["k3", "wout"], ["q0"], ["v1", "v2"]]


def slots_of(p, odd, last):
    full = ODD if odd else EVEN
    drop = set()
    if not odd and isinstance(p, int) and p == 0:
        drop.add("wout")
    if last:
        drop |= set(PROLOGUE) if odd else {"xt0", "xt1"}
    return [[u for u in slot if u not in drop] for slot in full]


def names_of(p, odd, last):
    return [u for slot in slots_of(p, odd, last) for u in slot]


def first_unit(p, odd, last):
    if isinstance(p, int) and p == 0:
        units, split = len(PROLOGUE), len(PROLOGUE)
    else:
        before = len(PROLOGUE) - 1
        units, split = before + 24 * p, before + 1 + 22 * p
    if odd:
        names = names_of(p, False, last)
        units, split = units + len(names), split + sum(u != "wout" for u in names)
    return units, split


def unit_count(p, odd, last, name):
    return first_unit(p, odd, last)[0] + names_of(p, odd, last).index(name) + 1


def split_count(p, odd, last, name):
    names = names_of(p, odd, last)
    return first_unit(p, odd, last)[1] + sum(u != "wout" for u in names[: names.index(name)]) + 1


def bank_of(p, odd, last, name):
    q = p if isinstance(p, int) else 1
    return (unit_count(q, odd, last, name) - 1) % UNIT_BANKS


def kv_count(p, odd, last, name):
    if odd or name == "q1":
        return unit_count(p, False, last, name)
    if isinstance(p, int) and p == 0:
        return PROLOGUE.index(name) + 1
    return unit_count(p - 1, True, False, name)


def build(nc, x, ctx, Wq, Wk, Wv, Wout, bout, Wr, rb, W1, W2, W3, Ws1, Ws2, Ws3, out):
    B, N, D = x.shape
    _, M, C = ctx.shape
    INNER = Wq.shape[1]
    HEADS, DH = 8, INNER // 8
    E, _, H = W1.shape
    TOKENS = B * N
    KR = 125
    KT = M // KR
    ME = M + 1
    CT = C - 128
    PAIRS = B // 2
    N2 = 2 * N
    assert KT * KR == M and CT == 64 and DH == 64 and D == 256 and B % 2 == 0
    QSCALE = DH ** -0.5
    RSCALE = D ** -0.5
    TILES = TOKENS // 128
    CHUNK = 512
    CHUNKS = TOKENS // CHUNK
    TC = CHUNK // 128
    MH = H // 128
    PIECES = 6
    assert CHUNKS == 7 and TILES == 28 and MH == 4

    xf = x.rearrange("b n d -> (b n) d")
    outf = out.rearrange("b n d -> (b n) d")
    x1_dram = nc.dram_tensor("x1_scratch", (TOKENS, D), F32, kind="Internal").ap()

    top = ExitStack()
    sb = lambda name, shape, dt=F32, at=top: at.enter_context(nc.sbuf_tensor(name, shape, dt))
    sem = lambda name: top.enter_context(nc.semaphore(name))

    with top:
        stage = sb("stage", [128, 4096])
        w_hi1 = sb("w_hi1", [128, PIECES * 512], F32R)
        w_lo1 = sb("w_lo1", [128, PIECES * 512], F32R)
        ident = sb("ident", [128, 128])
        bank = [top.enter_context(nc.psum_tensor(f"bank{i}", [128, 512], F32)) for i in range(8)]

        weights_in = [None, sem("weights_in1"), sem("weights_in2")]
        bout_in = sem("bout_in")
        x1_stored = [sem("x1_stored0"), sem("x1_stored1")]
        sw_hi, sw_lo = sem("sw_hi"), sem("sw_lo")

        def load_expert(eng, w1, w3, w2, s):
            eng.dma_start(stage[:, 0:1024].rearrange("p (k n) -> p k n", k=2),
                          w1.rearrange("(k p) n -> p k n", p=128)).then_inc(s, 16)
            eng.dma_start(stage[:, 1024:2048].rearrange("p (k n) -> p k n", k=2),
                          w3.rearrange("(k p) n -> p k n", p=128)).then_inc(s, 16)
            eng.dma_start(stage[:, 2048:3072].rearrange("p (k n) -> p k n", k=4),
                          w2.rearrange("(k p) n -> p k n", p=128)).then_inc(s, 16)

        attention(nc, locals())
        experts(nc, locals())


def attention(nc, g):
    (x, ctx, Wq, Wk, Wv, Wout, bout, Ws1, Ws2, Ws3) = (g[k] for k in "x ctx Wq Wk Wv Wout bout Ws1 Ws2 Ws3".split())
    (N, D, M, ME, INNER, HEADS, DH, KR, KT, CT, PAIRS, N2, QSCALE) = (
        g[k] for k in "N D M ME INNER HEADS DH KR KT CT PAIRS N2 QSCALE".split())
    (stage, w_hi1, w_lo1, ident, bank, weights_in, bout_in, x1_stored, sw_hi, sw_lo, x1_dram, load_expert, PIECES) = (
        g[k] for k in "stage w_hi1 w_lo1 ident bank weights_in bout_in x1_stored sw_hi sw_lo x1_dram load_expert PIECES".split())
    W1, W2, W3 = g["W1"], g["W2"], g["W3"]

    own = ExitStack()
    sb = lambda name, shape, dt=F32: own.enter_context(nc.sbuf_tensor(name, shape, dt))
    sem = lambda name: own.enter_context(nc.semaphore(name))
    with own:
        wq_hi, wq_lo = sb("wq_hi", [128, 2, INNER], F32R), sb("wq_lo", [128, 2, INNER], F32R)
        wk_hi, wk_lo = sb("wk_hi", [128, 2, INNER], F32R), sb("wk_lo", [128, 2, INNER], F32R)
        wv_hi, wv_lo = sb("wv_hi", [128, 2, INNER], F32R), sb("wv_lo", [128, 2, INNER], F32R)
        wo_hi, wo_lo = sb("wo_hi", [128, 4, D], F32R), sb("wo_lo", [128, 4, D], F32R)
        bout_sb = sb("bout_sb", [N, D])

        x_in = sb("x_in", [N, 2, D])
        xn = sb("xn", [N, 2, D])
        stats = sb("stats", [N, 2, 6])
        mean_var = sb("mean_var", [N, 2, 2])
        var_eps = sb("var_eps", [N, 2])
        minus_half, eps = sb("minus_half", [N, 2]), sb("eps", [N, 2])
        rstd = sb("rstd", [N, 2])
        xT_hi, xT_lo = sb("xT_hi", [128, 2, N2], F32R), sb("xT_lo", [128, 2, N2], F32R)
        ctx_in = [sb(f"ctx_in{i}", [KR, KT, 256]) for i in range(2)]
        cT_hi, cT_lo = sb("cT_hi", [128, ME], F32R), sb("cT_lo", [128, ME], F32R)
        cT_tail = sb("cT_tail", [128, ME], F32R)
        q_hi, q_lo = sb("q_hi", [128, HEADS, 2, N], F32R), sb("q_lo", [128, HEADS, 2, N], F32R)
        k_hi = [sb(f"k_hi{i}", [128, 4, ME], F32R) for i in range(2)]
        k_lo = [sb(f"k_lo{i}", [128, 4, ME], F32R) for i in range(2)]
        v_hi = [sb(f"v_hi{i}", [KR, KT, INNER], F32R) for i in range(2)]
        v_lo = [sb(f"v_lo{i}", [KR, KT, INNER], F32R) for i in range(2)]
        probs = sb("probs", [N, 4, M])
        neg_max, row_sum, inv_sum = sb("neg_max", [N, 16]), sb("row_sum", [N, 16]), sb("inv_sum", [N, 16])
        pT_hi = sb("pT_hi", [KR, 2, KT, 2, N], F32R)
        pT_lo = sb("pT_lo", [KR, 2, KT, 2, N], F32R)
        oT_hi = [sb(f"oT_hi{i}", [128, 4, N], F32R) for i in range(2)]
        oT_lo = [sb(f"oT_lo{i}", [128, 4, N], F32R) for i in range(2)]
        x_res = [sb(f"x_res{i}", [N, D]) for i in range(2)]
        x1 = [sb(f"x1_{i}", [N, D]) for i in range(2)]
        S_BANK, PT_BANK, O_BANK, U_BANK = bank[0:2], bank[2:4], bank[4], bank[5:8]

        x_loaded = sem("x_loaded")
        ctx_loaded = [sem("ctx_loaded0"), sem("ctx_loaded1")]
        res_loaded = [sem("res_loaded0"), sem("res_loaded1")]
        norm_consts, zeros_ready, ident_zero = sem("norm_consts"), sem("zeros_ready"), sem("ident_zero")
        ident_ready = sem("ident_ready")
        aw_in = {kind: sem(f"aw_in_{kind}") for kind in "kvqo"}
        aw_hi, aw_lo = sem("aw_hi"), sem("aw_lo")
        stats_done, var_ready, var_eps_ready, rstd_ready, xn_ready = (
            sem(n) for n in "stats_done var_ready var_eps_ready rstd_ready xn_ready".split())
        unit_made, unit_hi, unit_done = sem("unit_made"), sem("unit_hi"), sem("unit_done")
        res_biased = sem("res_biased")
        scores_made, max_ready, exp_ready, inv_ready, probs_ready = (
            sem(n) for n in "scores_made max_ready exp_ready inv_ready probs_ready".split())
        pT_made, pT_hi_ready, pT_ready = sem("pT_made"), sem("pT_hi_ready"), sem("pT_ready")
        o_made, o_hi_ready, o_ready = sem("o_made"), sem("o_hi_ready"), sem("o_ready")

        AW = [("k", 0), ("k", 1), ("v", 0), ("v", 1), ("q", 0), ("q", 1), ("o", 0), ("o", 1)]
        AW_LOADS = {"k": 48, "v": 48, "q": 32, "o": 16}
        HI = {"q": wq_hi, "k": wk_hi, "v": wv_hi, "o": wo_hi}
        LO = {"q": wq_lo, "k": wk_lo, "v": wv_lo, "o": wo_lo}

        def piece(t, kind, i):
            return t[:, 2 * i:2 * i + 2, :] if kind == "o" else t[:, i, :]

        def staged(n, kind):
            s = stage[:, n * 512:(n + 1) * 512]
            return s.rearrange("p (k n) -> p k n", k=2) if kind == "o" else s

        def heads_of(name, half):
            first = 4 * int(name[1]) + half
            return slice(first, first + 3, 2)

        def ps_q(ps, rows):
            return ps[rows, 0:2 * N2].rearrange("p (m b n) -> p m b n", m=2, b=2)

        def rounds(eng, body):
            body(0, False)
            with eng.Fori(1, PAIRS - 1) as p:
                body(p, False)
            body(PAIRS - 1, True)

        def ctx_rows(b):
            return ctx[bass.ds(b, 1), :, :].rearrange("o (t r) c -> r (o t) c", r=KR)

        def batch_of(b):
            return x[bass.ds(b, 1), :, :].rearrange("o r d -> (o r) d")

        def x_rows(b, n):
            return x[bass.ds(b, n), :, :].rearrange("b r d -> r b d")

        block = own.enter_context(nc.Block())

        @block.sync
        def _(sp):
            def load_ctx(b, i):
                rows = ctx_rows(b)
                sp.dma_start(ctx_in[i][:, :, 0:192], rows).then_inc(ctx_loaded[i], 16)
                sp.dma_start(ctx_in[i][:, :, 192:256], rows[:, :, 128:192]).then_inc(ctx_loaded[i], 16)

            def load_weight(w, n, kind, split_rows):
                sp.dma_start(stage[:, n * 512:(n + 1) * 512], w[0:128, :]).then_inc(aw_in[kind], 16)
                if split_rows:
                    sp.dma_start(stage[0:64, (n + 1) * 512:(n + 2) * 512], w[128:192, :]).then_inc(aw_in[kind], 16)
                    sp.dma_start(stage[64:128, (n + 1) * 512:(n + 2) * 512], w[128:192, :]).then_inc(aw_in[kind], 16)
                else:
                    sp.dma_start(stage[:, (n + 1) * 512:(n + 2) * 512], w[128:256, :]).then_inc(aw_in[kind], 16)

            load_ctx(0, 0)
            sp.dma_start(x_in[:], x_rows(0, 2)).then_inc(x_loaded, 16)
            load_weight(Wk, 0, "k", True)
            load_weight(Wv, 2, "v", True)
            load_weight(Wq, 4, "q", False)
            sp.dma_start(stage[:, 3072:4096].rearrange("p (k n) -> p k n", k=4),
                         Wout.rearrange("(k p) n -> p k n", p=128)).then_inc(aw_in["o"], 16)
            sp.dma_start(bout_sb[:], bout.rearrange("(o d) -> o d", o=1).to_broadcast([N, D])).then_inc(bout_in, 16)
            load_ctx(1, 1)
            sp.dma_start(x_res[0][:], x[0]).then_inc(res_loaded[0], 16)
            sp.dma_start(x_res[1][:], x[1]).then_inc(res_loaded[1], 16)
            sp.wait_ge(xn_ready, 1)
            sp.dma_start(x_in[:], x_rows(2, 2)).then_inc(x_loaded, 16)
            sp.wait_ge(unit_made, PROLOGUE.index("c1") + 1)
            load_ctx(2, 0)
            sp.wait_ge(aw_hi, len(AW))
            sp.wait_ge(aw_lo, len(AW))
            load_expert(sp, Ws1, Ws3, Ws2, weights_in[1])

            def store(b, i, count):
                sp.wait_ge(unit_done, count)
                sp.dma_start(x1_dram[bass.ds(b * N, N), :], x1[i][:]).then_inc(x1_stored[i], 16)

            def body(p, last):
                first = isinstance(p, int) and p == 0
                two_more = not isinstance(p, int) or p + 2 < PAIRS
                if not last:
                    sp.wait_ge(unit_made, unit_count(p, False, last, "c1"))
                    load_ctx(2 * p + 3, 1)
                if not first:
                    store(2 * p - 1, 1, unit_count(p, False, last, "wout"))
                    sp.dma_start(x_res[1][:], batch_of(2 * p + 1)).then_inc(res_loaded[1], 16)
                if two_more:
                    sp.wait_ge(xn_ready, p + 2)
                    sp.dma_start(x_in[:], x_rows(2 * p + 4, 2)).then_inc(x_loaded, 16)
                    sp.wait_ge(unit_made, unit_count(p, True, last, "c1"))
                    load_ctx(2 * p + 4, 0)
                store(2 * p, 0, unit_count(p, True, last, "wout"))
                if not last:
                    sp.dma_start(x_res[0][:], batch_of(2 * p + 2)).then_inc(res_loaded[0], 16)

            body(0, False)
            with sp.Fori(1, PAIRS - 2) as p:
                body(p, False)
            body(PAIRS - 2, False)
            body(PAIRS - 1, True)
            sp.wait_ge(unit_done, unit_count(PAIRS - 1, True, True, "wout") + 1)
            sp.dma_start(x1_dram[(2 * PAIRS - 1) * N:2 * PAIRS * N, :], x1[1][:]).then_inc(x1_stored[1], 16)
            for i in range(2):
                sp.wait_ge(x1_stored[i], 16 * PAIRS)
            sp.wait_ge(sw_hi, PIECES)
            sp.wait_ge(sw_lo, PIECES)
            load_expert(sp, W1[0], W3[0], W2[0], weights_in[2])

        @block.gpsimd
        def _(pool):
            pool.memset(ident[:], 0.0).then_inc(ident_zero, 1)
            pool.memset(minus_half[:], -0.5).then_inc(norm_consts, 1)
            pool.memset(eps[:], EPS).then_inc(norm_consts, 1)
            pool.wait_ge(ident_zero, 1)
            pool.affine_select(out=ident[:], in_=ident[:], compare_op=ALU.not_equal, fill=1.0, base=0,
                               pattern=[[-1, 128]], channel_multiplier=1).then_inc(ident_ready, 1)

            def rstd_of(n):
                pool.wait_ge(var_ready, n)
                pool.tensor_tensor(var_eps[:], mean_var[:, :, 1], eps[:], ALU.add).then_inc(var_eps_ready, 1)
                pool.wait_ge(var_eps_ready, n)
                pool.tensor_tensor(rstd[:], var_eps[:], minus_half[:], ALU.pow).then_inc(rstd_ready, 1)

            def add_bout(i, n):
                pool.wait_ge(res_loaded[i], 16 * n)
                pool.tensor_tensor(x_res[i][:], x_res[i][:], bout_sb[:], ALU.add).then_inc(res_biased, 1)

            pool.wait_ge(norm_consts, 2)
            rstd_of(1)
            pool.wait_ge(bout_in, 16)
            add_bout(0, 1)
            add_bout(1, 1)

            def body(p, last):
                for s in range(16):
                    pool.wait_ge(inv_ready, 16 * p + s + 1)
                    pool.tensor_tensor(probs[:, s % 4, :], probs[:, s % 4, :],
                                       inv_sum[:, s:s + 1].to_broadcast([N, M]), ALU.mult).then_inc(probs_ready, 1)
                    if s == 2 and not last:
                        rstd_of(p + 2)
                    if s in (1, 9) and not (isinstance(p, int) and p == 0):
                        add_bout(s // 8, p + 1)
                if isinstance(p, int) and p == 0:
                    pool.wait_ge(weights_in[1], 48)
                    for j in range(PIECES):
                        cols = slice(j * 512, (j + 1) * 512)
                        pool.wait_ge(sw_hi, j + 1)
                        pool.tensor_tensor(w_lo1[:, cols], stage[:, cols], w_hi1[:, cols].bitcast(F32),
                                           ALU.subtract).then_inc(sw_lo, 1)

            rounds(pool, body)

        @block.scalar
        def _(act):
            for n, (kind, i) in enumerate(AW):
                act.wait_ge(aw_in[kind], AW_LOADS[kind])
                act.activation(piece(HI[kind], kind, i), staged(n, kind), ACT.Copy,
                               scale=QSCALE if kind == "q" else 1.0).then_inc(aw_hi, 1)

            def unit(n_made, name, b, ps):
                act.wait_ge(unit_made, n_made)
                if name[0] == "x":
                    j = int(name[2])
                    act.activation(xT_hi[:, :, j * N:(j + 1) * N],
                                   ps[:, 0:2 * N].rearrange("p (k n) -> p k n", k=2), ACT.Copy).then_inc(unit_hi, 1)
                elif name == "c0":
                    act.activation(cT_hi[:, 0:M], ps[:, 0:M], ACT.Copy).then_inc(unit_hi, 1)
                elif name == "c1":
                    act.activation(cT_tail[:, 0:M], ps[:, 0:M], ACT.Copy).then_inc(unit_hi, 1)
                elif name[0] == "q":
                    for half in range(2):
                        rows, heads = slice(64 * half, 64 * half + 64), heads_of(name, half)
                        last = act.activation(q_hi[rows, heads, :, :], ps_q(ps, rows), ACT.Copy)
                    last.then_inc(unit_hi, 1)
                elif name[0] == "k":
                    act.activation(k_hi[b][:, int(name[1]), :], ps[:, 0:ME], ACT.Copy).then_inc(unit_hi, 1)
                elif name[0] == "v":
                    act.activation(v_hi[b][:, int(name[1]), :], ps[0:KR, :], ACT.Copy).then_inc(unit_hi, 1)

            for n, name in enumerate(PROLOGUE):
                unit(n + 1, name, 0, U_BANK[n % UNIT_BANKS])

            def o_part(a, j):
                act.wait_ge(o_made, a + 1)
                bk = O_BANK
                act.activation(oT_hi[j // 4][0:64, j % 4, :], bk[0:64, 0:N], ACT.Copy)
                act.activation(oT_hi[j // 4][64:128, j % 4, :], bk[64:128, N:N2], ACT.Copy).then_inc(o_hi_ready, 1)

            def slot(p, last, s, lead):
                gh = 16 * p + s
                odd = s // 8
                first = isinstance(p, int) and p == 0
                if lead:
                    act.wait_ge(max_ready, gh + 1)
                    wait(act, pT_made, gh - 3)
                    act.activation(probs[:, s % 4, :], S_BANK[s % 2][0:N, 0:M], ACT.Exp, bias=neg_max[:, s:s + 1],
                                   accum_out=row_sum[:, s:s + 1]).then_inc(exp_ready, 1)
                names = [u for u in slots_of(p, bool(odd), last)[s % 8]] if lead else []
                for n, name in enumerate(names):
                    if n > 0 or name == "wout":
                        continue
                    unit(unit_count(p, bool(odd), last, name), name, 1 - odd,
                         U_BANK[bank_of(p, bool(odd), last, name)])
                if not (first and s < 2) and s < 18:
                    t = s - 2
                    act.wait_ge(pT_made, gh - 1)
                    wait(act, o_made, 8 * p + t // 2 - 1)
                    act.activation(pT_hi[:, (t // 2) % 2, :, t % 2, :],
                                   PT_BANK[t % 2][0:KR, 0:KT * N].rearrange("p (t n) -> p t n", t=KT),
                                   ACT.Copy).then_inc(pT_hi_ready, 1)
                for n, name in enumerate(names):
                    if n > 0 and name != "wout":
                        unit(unit_count(p, bool(odd), last, name), name, 1 - odd,
                             U_BANK[bank_of(p, bool(odd), last, name)])
                if s % 2 == 0 and not (first and s < 4):
                    o_part(8 * p + s // 2 - 2, (s // 2 - 2) % 8)

            def body(p, last):
                for s in range(16):
                    slot(p, last, s, True)
                if isinstance(p, int) and p == 0:
                    act.wait_ge(weights_in[1], 48)
                    for j in range(PIECES):
                        cols = slice(j * 512, (j + 1) * 512)
                        act.activation(w_hi1[:, cols], stage[:, cols], ACT.Copy).then_inc(sw_hi, 1)

            rounds(act, body)
            for s in range(16, 19):
                slot(PAIRS - 1, True, s, False)

        @block.vector
        def _(dve):
            def statistics(n):
                dve.wait_ge(x_loaded, 16 * n)
                dve.bn_stats(stats[:, 0, :], x_in[:, 0, :])
                dve.bn_stats(stats[:, 1, :], x_in[:, 1, :]).then_inc(stats_done, 1)
                dve.wait_ge(x_loaded, 16)
                dve.wait_ge(stats_done, n)
                dve.bn_aggr(mean_var[:, 0, :], stats[:, 0, :])
                dve.bn_aggr(mean_var[:, 1, :], stats[:, 1, :]).then_inc(var_ready, 1)

            def normed(n):
                dve.wait_ge(rstd_ready, n)
                dve.wait_ge(var_ready, n)
                for j in range(2):
                    last = dve.tensor_scalar(xn[:, j, :], x_in[:, j, :], mean_var[:, j, 0:1], rstd[:, j:j + 1],
                                             ALU.subtract, ALU.mult)
                last.then_inc(xn_ready, 1)

            statistics(1)
            normed(1)
            for t in (q_hi, q_lo):
                for half in range(2):
                    dve.memset(t[64 * half:64 * half + 64, :, :, :].rearrange(
                        "p (m e) b n -> p m e (b n)", e=2)[:, :, 1 - half, :].bitcast(F32), 0.0).then_inc(zeros_ready, 1)
            dve.memset(wk_lo[64:128, 1, :].bitcast(F32), 0.0).then_inc(zeros_ready, 1)
            dve.memset(wv_lo[64:128, 1, :].bitcast(F32), 0.0).then_inc(zeros_ready, 1)

            for t in (cT_hi, cT_lo, cT_tail):
                dve.memset(t[:, M:ME].bitcast(F32), 0.0).then_inc(zeros_ready, 1)
            for n, (kind, i) in enumerate(AW):
                dve.wait_ge(aw_hi, n + 1)
                rows = slice(0, 64) if kind in "kv" and i == 1 else slice(0, 128)
                dve.scalar_tensor_tensor(piece(LO[kind], kind, i)[rows], staged(n, kind)[rows],
                                         QSCALE if kind == "q" else 1.0, piece(HI[kind], kind, i)[rows].bitcast(F32),
                                         ALU.mult, ALU.subtract).then_inc(aw_lo, 1)

            def unit(n_hi, name, b, ps):
                dve.wait_ge(unit_hi, n_hi)
                if name[0] == "x":
                    cols = slice(int(name[2]) * N, (int(name[2]) + 1) * N)
                    dve.tensor_tensor(xT_lo[:, :, cols], ps[:, 0:2 * N].rearrange("p (k n) -> p k n", k=2),
                                      xT_hi[:, :, cols].bitcast(F32), ALU.subtract).then_inc(unit_done, 1)
                elif name == "c0":
                    dve.tensor_tensor(cT_lo[:, 0:M], ps[:, 0:M], cT_hi[:, 0:M].bitcast(F32), ALU.subtract).then_inc(unit_done, 1)
                elif name == "c1":
                    dve.tensor_tensor(cT_tail[64:128, 0:M], ps[64:128, 0:M], cT_tail[64:128, 0:M].bitcast(F32),
                                      ALU.subtract).then_inc(unit_done, 1)
                elif name[0] == "q":
                    for half in range(2):
                        rows, heads = slice(64 * half, 64 * half + 64), heads_of(name, half)
                        last = dve.tensor_tensor(q_lo[rows, heads, :, :], ps_q(ps, rows),
                                                 q_hi[rows, heads, :, :].bitcast(F32), ALU.subtract)
                    last.then_inc(unit_done, 1)
                elif name[0] == "k":
                    m = int(name[1])
                    dve.tensor_tensor(k_lo[b][:, m, :], ps[:, 0:ME], k_hi[b][:, m, :].bitcast(F32),
                                      ALU.subtract).then_inc(unit_done, 1)
                elif name[0] == "v":
                    t = int(name[1])
                    dve.tensor_tensor(v_lo[b][:, t, :], ps[0:KR, :], v_hi[b][:, t, :].bitcast(F32),
                                      ALU.subtract).then_inc(unit_done, 1)

            def residual(count, i, n_res, n_store, ps):
                dve.wait_ge(unit_made, count)
                dve.wait_ge(res_biased, n_res)
                wait(dve, x1_stored[i], 16 * n_store)
                dve.tensor_tensor(x1[i][:], ps[0:N, 0:D], x_res[i][:], ALU.add).then_inc(unit_done, 1)

            for n, name in enumerate(PROLOGUE):
                unit(n + 1, name, 0, U_BANK[n % UNIT_BANKS])

            def run(p, odd, last, name):
                ps = U_BANK[bank_of(p, odd, last, name)]
                if name == "wout":
                    residual(unit_count(p, odd, last, name), 0 if odd else 1,
                             2 * p + 1 if odd else 2 * p, p if odd else p - 1, ps)
                else:
                    unit(split_count(p, odd, last, name), name, 0 if odd else 1, ps)

            def slot(p, last, s, lead):
                gh = 16 * p + s
                odd = bool(s // 8)
                first = isinstance(p, int) and p == 0
                if lead:
                    dve.wait_ge(scores_made, gh + 1)
                    dve.tensor_reduce(neg_max[:, s:s + 1], S_BANK[s % 2][0:N, 0:M], AX.X, ALU.max,
                                      negate=True).then_inc(max_ready, 1)
                if s == 0 and not first:
                    for name in ODD[7][1:]:
                        run(p - 1, True, False, name)
                elif 0 < s <= 16 and not (last and s == 16):
                    was_odd = (s - 1) // 8 == 1
                    for name in slots_of(p, was_odd, last)[(s - 1) % 8][1:]:
                        run(p, was_odd, last, name)
                if lead:
                    dve.wait_ge(exp_ready, gh + 1)
                    dve.reciprocal(inv_sum[:, s:s + 1], row_sum[:, s:s + 1]).then_inc(inv_ready, 1)
                if s % 2 == 1 and not (first and s < 5):
                    j = ((s - 1) // 2 - 2) % 8
                    dve.wait_ge(o_hi_ready, 8 * p + (s - 1) // 2 - 1)
                    dve.tensor_tensor(oT_lo[j // 4][0:64, j % 4, :], O_BANK[0:64, 0:N],
                                      oT_hi[j // 4][0:64, j % 4, :].bitcast(F32), ALU.subtract)
                    dve.tensor_tensor(oT_lo[j // 4][64:128, j % 4, :], O_BANK[64:128, N:N2],
                                      oT_hi[j // 4][64:128, j % 4, :].bitcast(F32), ALU.subtract).then_inc(o_ready, 1)
                names = slots_of(p, odd, last)[s % 8] if lead else []
                if names:
                    run(p, odd, last, names[0])
                if not (first and s < 2) and s < 18:
                    t = s - 2
                    dve.wait_ge(pT_hi_ready, gh - 1)
                    dve.tensor_tensor(pT_lo[:, (t // 2) % 2, :, t % 2, :],
                                      PT_BANK[t % 2][0:KR, 0:KT * N].rearrange("p (t n) -> p t n", t=KT),
                                      pT_hi[:, (t // 2) % 2, :, t % 2, :].bitcast(F32),
                                      ALU.subtract).then_inc(pT_ready, 1)
                if s == 1 and lead and not last:
                    statistics(p + 2)
                if s == 4 and lead and not last:
                    normed(p + 2)

            def body(p, last):
                for s in range(16):
                    slot(p, last, s, True)

            rounds(dve, body)
            for s in range(16, 20):
                slot(PAIRS - 1, True, s, False)
            n = unit_count(PAIRS - 1, True, True, "wout") + 1
            residual(n, 1, 2 * PAIRS, PAIRS - 1, U_BANK[(n - 1) % UNIT_BANKS])

        @block.tensor
        def _(pe):
            def product(o, pairs):
                for n, (lhsT, rhs) in enumerate(pairs):
                    mm = pe.matmul(o, lhsT, rhs, start=(n == 0), stop=(n == len(pairs) - 1))
                return mm

            def unit(count, name, b, ps):
                wait(pe, unit_done, count - UNIT_BANKS)
                if name[0] == "x":
                    j = int(name[2])
                    for k in range(2):
                        mm = pe.transpose(ps[:, k * N:(k + 1) * N], xn[:, j, k * 128:(k + 1) * 128], ident[0:N, 0:N])
                elif name[0] == "c":
                    c = int(name[1]) * 128
                    for t in range(KT):
                        mm = pe.transpose(ps[:, t * KR:(t + 1) * KR], ctx_in[b][:, t, c:c + 128], ident[0:KR, 0:KR])
                elif name[0] == "q":
                    for m in range(2):
                        cols = slice((2 * int(name[1]) + m) * 128, (2 * int(name[1]) + m + 1) * 128)
                        mm = product(ps[:, m * N2:(m + 1) * N2],
                                     [(w[:, k, cols], v[:, k, :]) for k in range(2)
                                      for w, v in ((wq_hi, xT_hi), (wq_hi, xT_lo), (wq_lo, xT_hi))])
                elif name[0] == "k":
                    cols = slice(int(name[1]) * 128, int(name[1]) * 128 + 128)
                    mm = product(ps[:, 0:ME], [(wk_hi[:, 0, cols], cT_hi[:]), (wk_hi[:, 0, cols], cT_lo[:]),
                                              (wk_lo[:, 0, cols], cT_hi[:]), (wk_hi[:, 1, cols], cT_tail[:]),
                                              (wk_lo[:, 1, cols], cT_tail[:])])
                elif name[0] == "v":
                    r = slice(int(name[1]) * KR, (int(name[1]) + 1) * KR)
                    mm = product(ps[0:KR, :], [(cT_hi[:, r], wv_hi[:, 0, :]), (cT_lo[:, r], wv_hi[:, 0, :]),
                                               (cT_hi[:, r], wv_lo[:, 0, :]), (cT_tail[:, r], wv_hi[:, 1, :]),
                                               (cT_tail[:, r], wv_lo[:, 1, :])])
                elif name == "wout":
                    mm = product(ps[0:N, 0:D], [(o[b][:, k, :], w[:, k, :]) for k in range(4)
                                                for o, w in ((oT_hi, wo_hi), (oT_lo, wo_hi), (oT_hi, wo_lo))])
                mm.then_inc(unit_made, 1)

            pe.wait_ge(ident_ready, 1)
            for n, name in enumerate(PROLOGUE):
                if name == "xt0":
                    pe.wait_ge(xn_ready, 1)
                if name == "c0":
                    pe.wait_ge(ctx_loaded[0], 32)
                if name == "k0":
                    pe.wait_ge(zeros_ready, 9)
                    pe.wait_ge(aw_lo, 2)
                    pe.wait_ge(unit_done, n)
                if name == "v0":
                    pe.wait_ge(aw_lo, 4)
                if name == "q0":
                    pe.wait_ge(aw_lo, 6)
                    pe.wait_ge(unit_done, PROLOGUE.index("xt1") + 1)
                unit(n + 1, name, 0, U_BANK[n % UNIT_BANKS])

            def slot(p, last, s, lead):
                gh = 16 * p + s
                odd = bool(s // 8)
                first = isinstance(p, int) and p == 0
                h = s % 8
                if lead:
                    if s in (0, 4):
                        pe.wait_ge(unit_done, kv_count(p, False, last, f"q{s // 4}"))
                    pe.wait_ge(unit_done, kv_count(p, odd, last, f"k{h // 2}"))
                    wait(pe, exp_ready, gh - 1)
                    i, m = int(odd), h // 2
                    product(S_BANK[s % 2][0:N, 0:ME], [(q_hi[:, h, i, :], k_hi[i][:, m, :]),
                                                      (q_hi[:, h, i, :], k_lo[i][:, m, :]),
                                                      (q_lo[:, h, i, :], k_hi[i][:, m, :])]).then_inc(scores_made, 1)
                names = slots_of(p, odd, last)[s % 8] if lead else []

                def run(name):
                    count = unit_count(p, odd, last, name)
                    if name == "xt0":
                        pe.wait_ge(xn_ready, p + 2)
                    if name == "c0":
                        pe.wait_ge(ctx_loaded[0 if odd else 1], 32 * (p + 2 if odd else p + 1))
                    if name == "k0":
                        pe.wait_ge(unit_done, unit_count(p, odd, last, "c1"))
                    if name == "q0":
                        pe.wait_ge(unit_done, unit_count(p, False, last, "xt1"))
                    if name == "wout" and first:
                        pe.wait_ge(aw_lo, 8)
                    if name == "wout":
                        pe.wait_ge(o_ready, 8 * p + 4 if odd else 8 * p)
                    unit(count, name, 0 if odd else 1, U_BANK[bank_of(p, odd, last, name)])

                if names:
                    run(names[0])
                if not (first and s < 2) and s < 18:
                    t = s - 2
                    pe.wait_ge(probs_ready, gh - 1)
                    wait(pe, pT_ready, gh - 3)
                    for kt in range(KT):
                        mm = pe.transpose(PT_BANK[t % 2][0:KR, kt * N:(kt + 1) * N],
                                          probs[:, t % 4, kt * KR:(kt + 1) * KR], ident[0:N, 0:N])
                    mm.then_inc(pT_made, 1)
                for name in names[1:]:
                    run(name)
                if s % 2 == 0 and not (first and s < 4):
                    a = 8 * p + s // 2 - 2
                    j = (s // 2 - 2) % 8
                    i, m = j // 4, j % 4
                    pe.wait_ge(pT_ready, 2 * a + 2)
                    if m == 0:
                        pe.wait_ge(unit_done, kv_count(p, i == 1, last, "v2"))
                    wait(pe, o_ready, a)
                    vh, vl, cols = v_hi[i], v_lo[i], slice(m * 128, (m + 1) * 128)
                    pt = [t[:, j % 2, :, :, :].rearrange("p t e n -> p t (e n)") for t in (pT_hi, pT_lo)]
                    product(O_BANK[:, 0:N2],
                            [(v[:, kt, cols], w[:, kt, :]) for kt in range(KT)
                             for v, w in ((vh, pt[0]), (vh, pt[1]), (vl, pt[0]))]).then_inc(o_made, 1)

            def body(p, last):
                for s in range(16):
                    slot(p, last, s, True)

            rounds(pe, body)
            for s in range(16, 19):
                slot(PAIRS - 1, True, s, False)
            n = unit_count(PAIRS - 1, True, True, "wout") + 1
            pe.wait_ge(o_ready, 8 * PAIRS)
            unit(n, "wout", 1, U_BANK[(n - 1) % UNIT_BANKS])


def experts(nc, g):
    (W1, W2, W3, Wr, rb, outf, x1_dram) = (g[k] for k in "W1 W2 W3 Wr rb outf x1_dram".split())
    (D, E, H, TILES, CHUNK, CHUNKS, TC, MH, PIECES, RSCALE) = (
        g[k] for k in "D E H TILES CHUNK CHUNKS TC MH PIECES RSCALE".split())
    (stage, w_hi1, w_lo1, ident, bank, weights_in, load_expert) = (
        g[k] for k in "stage w_hi1 w_lo1 ident bank weights_in load_expert".split())

    own = ExitStack()
    sb = lambda name, shape, dt=F32: own.enter_context(nc.sbuf_tensor(name, shape, dt))
    sem = lambda name: own.enter_context(nc.semaphore(name))
    with own:
        w_hi = [sb("w_hi0", [128, PIECES * 512], F32R), w_hi1]
        w_lo = [sb("w_lo0", [128, PIECES * 512], F32R), w_lo1]
        acc = sb("acc", [128, TILES, D])
        xn = sb("xn2", [128, TC, D])
        stats = sb("stats2", [128, TC, 6])
        mean_var = sb("mean_var2", [128, TC, 2])
        var_eps, rstd, minus_half = sb("var_eps2", [128, TC]), sb("rstd2", [128, TC]), sb("minus_half2", [128, TC])
        xT_hi, xT_lo = sb("x2T_hi", [128, 2, TILES * 128], F32R), sb("x2T_lo", [128, 2, TILES * 128], F32R)
        hT_hi = [sb(f"hT_hi{i}", [128, MH, CHUNK], F32R) for i in range(2)]
        hT_lo = [sb(f"hT_lo{i}", [128, MH, CHUNK], F32R) for i in range(2)]
        tanh = sb("tanh", [128, 2, CHUNK])
        gate = sb("gate", [128, CHUNK])
        hidden = sb("hidden", [128, 2, CHUNK])
        wr, rb_sb = sb("wr", [128, 2, E]), sb("rb_sb", [128, E])
        wr_hi, wr_lo = sb("wr_hi", [128, 2, E], F32R), sb("wr_lo", [128, 2, E], F32R)
        logits = sb("logits", [128, TILES, E])
        biased = sb("biased", [128, TILES, E])
        top = sb("top", [128, TILES, 8])
        top_at = sb("top_at", [128, TILES, 8], U32)
        top_atf = sb("top_atf", [128, TILES, 2])
        iota = sb("iota", [128, E])
        pick = sb("pick", [128, 2, TILES, E])
        picked = sb("picked", [128, 2, TILES, E])
        chosen = sb("chosen", [128, 2, TILES])
        most, total, total_inv = sb("most", [128, TILES]), sb("total", [128, TILES]), sb("total_inv", [128, TILES])
        share = sb("share", [128, 1 + E, TILES])
        H_BANK, Y_BANK, X_BANK = (bank[0:2], bank[2:4]), bank[4:6], bank[6:8]

        x1_loaded = [sem(f"x1_loaded{c}") for c in range(CHUNKS)]
        router_in = sem("router_in")
        consts = sem("consts2")
        stats_done, var_ready, var_eps_ready, rstd_ready, xn_ready = (
            sem(n + "2") for n in "stats_done var_ready var_eps_ready rstd_ready xn_ready".split())
        xT_made, xT_hi_ready, xT_ready = sem("xT_made"), sem("xT_hi_ready"), sem("xT_ready")
        wr_hi_ready, wr_ready = sem("wr_hi_ready"), sem("wr_ready")
        logits_made, logits_ready = sem("logits_made"), sem("logits_ready")
        route = sem("route")
        chosen_ready, chosen_exp = sem("chosen_ready"), sem("chosen_exp")
        a3_made, a1_made = sem("a3_made"), sem("a1_made")
        tanh_ready, gate_ready, hidden_ready = sem("tanh_ready"), sem("gate_ready"), sem("hidden_ready")
        h_hi_ready, h_ready = sem("h_hi_ready"), sem("h_ready")
        y_made, y_added = sem("y_made"), sem("y_added")
        piece_hi, piece_lo = sem("piece_hi"), sem("piece_lo")
        out_stored = sem("out_stored")
        LAST_PAIR = E // 2 - 1

        def shared(step):
            for c in range(CHUNKS):
                step(c, c, 1, None, c, c > 0)

        def routed(eng, step, between=None):
            def pair(i, last):
                for odd in range(2):
                    n = CHUNKS + 2 * CHUNKS * i + CHUNKS * odd
                    e = 2 * i + odd
                    step(n, 0, odd, e, 0, True, last)
                    with eng.Fori(0, 3) as j:
                        for k in range(2):
                            step(n + 2 * j + 1 + k, 2 * j + 1 + k, odd, e, 1 + k, True, last)

            with eng.Fori(0, LAST_PAIR) as i:
                pair(i, False)
            pair(LAST_PAIR, True)

        def parity(n_static):
            return n_static % 2

        block = own.enter_context(nc.Block())

        @block.sync
        def _(sp):
            x1_rows = x1_dram.rearrange("(t p) d -> p t d", p=128)
            for c in range(CHUNKS):
                sp.dma_start(acc[:, c * TC:(c + 1) * TC, :], x1_rows[:, c * TC:(c + 1) * TC, :]).then_inc(x1_loaded[c], 16)
                if c == 0:
                    sp.dma_start(wr[:], Wr.rearrange("(k p) e -> p k e", p=128)).then_inc(router_in, 16)
                    sp.dma_start(rb_sb[:], rb.rearrange("(o e) -> o e", o=1).to_broadcast([128, E])).then_inc(router_in, 16)
            def fetch(e, n):
                sp.wait_ge(piece_hi, PIECES * n)
                sp.wait_ge(piece_lo, PIECES * n)
                load_expert(sp, *(w[bass.ds(e, 1), :, :].rearrange("o d h -> (o d) h") for w in (W1, W3, W2)),
                            weights_in[2])

            with sp.Fori(1, E) as e:
                fetch(e, e)
            out_rows = outf.rearrange("(t p) d -> p t d", p=128)
            for c in range(CHUNKS):
                sp.wait_ge(y_added, TILES * E + TC * (c + 1))
                sp.dma_start(out_rows[:, c * TC:(c + 1) * TC, :], acc[:, c * TC:(c + 1) * TC, :]).then_inc(out_stored, 16)
            sp.wait_ge(out_stored, 16 * CHUNKS)

        @block.gpsimd
        def _(pool):
            pool.memset(minus_half[:], -0.5).then_inc(consts, 1)
            pool.iota(iota[:], pattern=[[1, E]], base=0, channel_multiplier=0,
                      allow_small_or_imprecise_dtypes=True).then_inc(consts, 1)
            pool.memset(share[:, 0, :], 1.0).then_inc(consts, 1)
            pool.wait_ge(consts, 3)

            def rstd_of(c):
                pool.wait_ge(var_ready, c + 1)
                pool.tensor_scalar(var_eps[:], mean_var[:, :, 1], EPS, 1.0, ALU.add, ALU.mult).then_inc(var_eps_ready, 1)
                pool.wait_ge(var_eps_ready, c + 1)
                pool.tensor_tensor(rstd[:], var_eps[:], minus_half[:], ALU.pow).then_inc(rstd_ready, 1)

            def lo_of_hidden(n, s):
                for m in range(MH):
                    pool.wait_ge(h_hi_ready, MH * n + m + 1)
                    pool.tensor_tensor(hT_lo[s][:, m, :], hidden[:, m % 2, :], hT_hi[s][:, m, :].bitcast(F32),
                                       ALU.subtract).then_inc(h_ready, 1)

            def lo_of_piece(n, j, buf):
                pool.wait_ge(piece_hi, PIECES * n + j + 1)
                cols = bass.ds(j * 512, 512)
                pool.tensor_tensor(w_lo[buf][:, cols], stage[:, cols], w_hi[buf][:, cols].bitcast(F32),
                                   ALU.subtract).then_inc(piece_lo, 1)

            rstd_of(0)
            for c in range(CHUNKS):
                if c + 1 < CHUNKS:
                    rstd_of(c + 1)
                lo_of_hidden(c, c % 2)
                if c > 0:
                    lo_of_piece(0, c - 1, 0)

            def step(n, c, buf, e, k, prev, last):
                lo_of_hidden(n, (CHUNKS + CHUNKS * buf + k) % 2)
                if k > 0 and not (last and buf == 1):
                    lo_of_piece(e + 1, c - 1, 1 - buf)

            routed(pool, step)

        @block.scalar
        def _(act):
            act.wait_ge(router_in, 32)
            act.activation(wr_hi[:], wr[:], ACT.Copy).then_inc(wr_hi_ready, 1)

            def hi_of_x(c):
                for k in range(2):
                    act.wait_ge(xT_made, 2 * c + k + 1)
                    act.activation(xT_hi[:, k, c * CHUNK:(c + 1) * CHUNK], X_BANK[k][:], ACT.Copy).then_inc(xT_hi_ready, 1)

            def units(n, s):
                for m in range(MH):
                    act.wait_ge(a3_made, MH * n + m + 1)
                    act.activation(tanh[:, m % 2, :], H_BANK[0][m % 2][:], ACT.Tanh, scale=0.5).then_inc(tanh_ready, 1)
                    act.wait_ge(hidden_ready, MH * n + m + 1)
                    act.activation(hT_hi[s][:, m, :], hidden[:, m % 2, :], ACT.Copy).then_inc(h_hi_ready, 1)

            def hi_of_piece(n, j, buf):
                if not isinstance(j, int) or j == 0:
                    act.wait_ge(weights_in[2], 48 * (n + 1))
                cols = bass.ds(j * 512, 512)
                act.activation(w_hi[buf][:, cols], stage[:, cols], ACT.Copy).then_inc(piece_hi, 1)

            hi_of_x(0)
            for c in range(CHUNKS):
                units(c, c % 2)
                if c > 0:
                    hi_of_piece(0, c - 1, 0)
                if c + 1 < CHUNKS:
                    hi_of_x(c + 1)
            act.wait_ge(chosen_ready, 1)
            act.activation(chosen[:], chosen[:], ACT.Exp).then_inc(chosen_exp, 1)

            def step(n, c, buf, e, k, prev, last):
                units(n, (CHUNKS + CHUNKS * buf + k) % 2)
                if k > 0 and not (last and buf == 1):
                    if k == 1:
                        act.wait_ge(y_made, TILES * (e + 1))
                    hi_of_piece(e + 1, c - 1, 1 - buf)

            routed(act, step)

        @block.vector
        def _(dve):
            dve.wait_ge(wr_hi_ready, 1)
            dve.tensor_tensor(wr_lo[:], wr[:], wr_hi[:].bitcast(F32), ALU.subtract).then_inc(wr_ready, 1)

            def statistics(c):
                dve.wait_ge(x1_loaded[c], 16)
                for t in range(TC):
                    last = dve.bn_stats(stats[:, t, :], acc[:, c * TC + t, :])
                last.then_inc(stats_done, 1)
                dve.wait_ge(stats_done, c + 1)
                for t in range(TC):
                    last = dve.bn_aggr(mean_var[:, t, :], stats[:, t, :])
                last.then_inc(var_ready, 1)

            def normed(c):
                dve.wait_ge(rstd_ready, c + 1)
                wait(dve, xT_made, 2 * c)
                for t in range(TC):
                    last = dve.tensor_scalar(xn[:, t, :], acc[:, c * TC + t, :], mean_var[:, t, 0:1],
                                             rstd[:, t:t + 1], ALU.subtract, ALU.mult)
                last.then_inc(xn_ready, 1)

            def lo_of_x(c):
                for k in range(2):
                    cols = slice(c * CHUNK, (c + 1) * CHUNK)
                    dve.wait_ge(xT_hi_ready, 2 * c + k + 1)
                    dve.tensor_tensor(xT_lo[:, k, cols], X_BANK[k][:], xT_hi[:, k, cols].bitcast(F32),
                                      ALU.subtract).then_inc(xT_ready, 1)

            def link(count):
                dve.wait_ge(route, count)

            def take_logits(c):
                t = slice(c * TC, (c + 1) * TC)
                dve.wait_ge(logits_made, c + 1)
                dve.tensor_scalar(logits[:, t, :], X_BANK[0][:, 0:TC * E].rearrange("p (t e) -> p t e", e=E),
                                  RSCALE, None, ALU.mult).then_inc(logits_ready, 1)
                dve.wait_ge(logits_ready, c + 1)
                dve.tensor_tensor(biased[:, t, :], logits[:, t, :],
                                  rb_sb[:].rearrange("p (o e) -> p o e", o=1).to_broadcast([128, TC, E]),
                                  ALU.add).then_inc(route, 1)

            def routing(c):
                link(3 * c + 1)
                for i in range(c * TC, (c + 1) * TC):
                    last = dve.max(top[:, i, :], biased[:, i, :])
                last.then_inc(route, 1)
                link(3 * c + 2)
                for i in range(c * TC, (c + 1) * TC):
                    last = dve.max_index(top_at[:, i, :], top[:, i, :], biased[:, i, :])
                last.then_inc(route, 1)

            def units(n, s):
                for m in range(MH):
                    count = MH * n + m + 1
                    dve.wait_ge(tanh_ready, count)
                    wait(dve, hidden_ready, count - 1)
                    dve.scalar_tensor_tensor(gate[:], tanh[:, m % 2, :], 1.0, H_BANK[0][m % 2][:],
                                             ALU.add, ALU.mult).then_inc(gate_ready, 1)
                    dve.wait_ge(gate_ready, count)
                    dve.wait_ge(a1_made, count)
                    wait(dve, h_ready, count - 2)
                    dve.scalar_tensor_tensor(hidden[:, m % 2, :], gate[:], 0.5, H_BANK[1][m % 2][:],
                                             ALU.mult, ALU.mult).then_inc(hidden_ready, 1)

            def add_y(n, c, e):
                for t in range(TC):
                    dve.wait_ge(y_made, TC * n + t + 1)
                    at = bass.ds(c * TC + t, 1)
                    dst = acc[:, at, :].rearrange("p o d -> p (o d)")
                    dve.scalar_tensor_tensor(dst, Y_BANK[t % 2][:, 0:D],
                                             share[:, bass.ds(e, 1), at].rearrange("p a b -> p (a b)"), dst,
                                             ALU.mult, ALU.add).then_inc(y_added, 1)

            def shares():
                n = 3 * CHUNKS
                link(n)
                dve.tensor_copy(top_atf[:], top_at[:, :, 0:2]).then_inc(route, 1)
                link(n + 1)
                all_e = iota[:].rearrange("p (o e) -> p o e", o=1).to_broadcast([128, TILES, E])
                for i in range(2):
                    last = dve.tensor_tensor(pick[:, i], all_e, top_atf[:, :, i:i + 1].to_broadcast([128, TILES, E]),
                                             ALU.is_equal)
                last.then_inc(route, 1)
                link(n + 2)
                for i in range(2):
                    last = dve.tensor_tensor(picked[:, i], pick[:, i], logits[:], ALU.mult)
                last.then_inc(route, 1)
                link(n + 3)
                for i in range(2):
                    last = dve.tensor_reduce(chosen[:, i, :], picked[:, i], AX.X, ALU.add)
                last.then_inc(route, 1)
                link(n + 4)
                dve.tensor_tensor(most[:], chosen[:, 0, :], chosen[:, 1, :], ALU.max).then_inc(route, 1)
                link(n + 5)
                for i in range(2):
                    last = dve.tensor_tensor(chosen[:, i, :], chosen[:, i, :], most[:], ALU.subtract)
                last.then_inc(chosen_ready, 1)
                dve.wait_ge(chosen_exp, 1)
                dve.tensor_tensor(total[:], chosen[:, 0, :], chosen[:, 1, :], ALU.add).then_inc(route, 1)
                link(n + 6)
                dve.reciprocal(total_inv[:], total[:]).then_inc(route, 1)
                link(n + 7)
                for i in range(2):
                    last = dve.tensor_tensor(chosen[:, i, :], chosen[:, i, :], total_inv[:], ALU.mult)
                last.then_inc(route, 1)
                link(n + 8)
                for i in range(2):
                    last = dve.tensor_tensor(picked[:, i], pick[:, i],
                                             chosen[:, i, :].rearrange("p (t o) -> p t o", o=1).to_broadcast([128, TILES, E]),
                                             ALU.mult)
                last.then_inc(route, 1)
                link(n + 9)
                dve.tensor_tensor(share[:, 1:, :].rearrange("p e t -> p t e"), picked[:, 0], picked[:, 1],
                                  ALU.add).then_inc(route, 1)
                link(n + 10)

            statistics(0)
            normed(0)
            lo_of_x(0)
            for c in range(CHUNKS):
                if c + 1 < CHUNKS:
                    statistics(c + 1)
                    normed(c + 1)
                take_logits(c)
                units(c, c % 2)
                if c + 1 < CHUNKS:
                    lo_of_x(c + 1)
                routing(c)
                if c == 0:
                    dve.wait_ge(consts, 3)
                else:
                    add_y(c - 1, c - 1, 0)

            def step(n, c, buf, e, k, prev, last):
                units(n, None)
                if k == 0:
                    add_y(n - 1, CHUNKS - 1, e)
                else:
                    add_y(n - 1, c - 1, e + 1)

            shares()
            routed(dve, step)
            add_y(CHUNKS * (E + 1) - 1, CHUNKS - 1, E)

        @block.tensor
        def _(pe):
            def product(o, pairs):
                for n, (lhsT, rhs) in enumerate(pairs):
                    mm = pe.matmul(o, lhsT, rhs, start=(n == 0), stop=(n == len(pairs) - 1))
                return mm

            def transposed(c):
                pe.wait_ge(xn_ready, c + 1)
                wait(pe, xT_ready, 2 * c)
                wait(pe, logits_ready, c)
                for k in range(2):
                    for t in range(TC):
                        mm = pe.transpose(X_BANK[k][:, t * 128:(t + 1) * 128], xn[:, t, k * 128:(k + 1) * 128], ident[:])
                    mm.then_inc(xT_made, 1)

            def router(c):
                for t in range(TC):
                    tok = slice((c * TC + t) * 128, (c * TC + t + 1) * 128)
                    mm = product(X_BANK[0][:, t * E:(t + 1) * E],
                                 [(v[:, k, tok], w[:, k, :]) for k in range(2)
                                  for v, w in ((xT_hi, wr_hi), (xT_lo, wr_hi), (xT_hi, wr_lo))])
                mm.then_inc(logits_made, 1)

            def up(n, c, buf):
                tok = bass.ds(c * CHUNK, CHUNK)
                for m in range(MH):
                    wait(pe, hidden_ready, MH * n + m - 1)
                    for o, base, made in ((H_BANK[0], 1024, a3_made), (H_BANK[1], 0, a1_made)):
                        cols = [slice(base + k * 512 + m * 128, base + k * 512 + m * 128 + 128) for k in range(2)]
                        product(o[m % 2][:], [(w[:, cols[k]], v[:, k, tok]) for k in range(2)
                                              for w, v in ((w_hi[buf], xT_hi), (w_hi[buf], xT_lo), (w_lo[buf], xT_hi))]
                                ).then_inc(made, 1)

            def down(n, buf, s):
                pe.wait_ge(h_ready, MH * (n + 1))
                for t in range(TC):
                    wait(pe, y_added, TC * n + t - 1)
                    tok = slice(t * 128, (t + 1) * 128)
                    w2 = [slice(2048 + k * D, 2048 + (k + 1) * D) for k in range(MH)]
                    product(Y_BANK[t % 2][:, 0:D],
                            [(h[s][:, k, tok], w[buf][:, w2[k]]) for k in range(MH)
                             for h, w in ((hT_hi, w_hi), (hT_lo, w_hi), (hT_hi, w_lo))]).then_inc(y_made, 1)

            transposed(0)
            pe.wait_ge(wr_ready, 1)
            for c in range(CHUNKS):
                pe.wait_ge(xT_ready, 2 * c + 2)
                router(c)
                up(c, c, 1)
                if c + 1 < CHUNKS:
                    transposed(c + 1)
                if c > 0:
                    down(c - 1, 1, (c - 1) % 2)

            def step(n, c, buf, e, k, prev, last):
                if k == 0:
                    pe.wait_ge(piece_lo, PIECES * (e + 1))
                s = (CHUNKS + CHUNKS * buf + k) % 2
                up(n, c, buf)
                down(n - 1, 1 - buf if k == 0 else buf, 1 - s)

            routed(pe, step)
            down(CHUNKS * (E + 1) - 1, 1, (2 * CHUNKS + CHUNKS - 1) % 2)


_INS = ['x', 'ctx_768', 'L0_xattn_Wq', 'L0_xattn_Wk', 'L0_xattn_Wv', 'L0_xattn_Wout', 'L0_xattn_bout',
        'L0_ffn_Wr', 'L0_ffn_rb', 'L0_ffn_W1', 'L0_ffn_W2', 'L0_ffn_W3', 'L0_ffn_Ws1', 'L0_ffn_Ws2', 'L0_ffn_Ws3']


def kernel(**inputs):
    import numpy as _np
    import concourse.bacc as _bacc
    from concourse import mybir as _mybir
    from concourse.bass_utils import run_bass_kernel_spmd as _run

    nc = _bacc.Bacc("TRN2", target_bir_lowering=False, num_devices=1)
    arrays, args = {}, []
    for name in _INS:
        a = _np.ascontiguousarray(inputs[name])
        arrays[f"in_{name}"] = a
        args.append(nc.dram_tensor(f"in_{name}", a.shape, _mybir.dt.from_np(a.dtype), kind="ExternalInput").ap())
    out = nc.dram_tensor("out_0", inputs["x"].shape, _mybir.dt.float32, kind="ExternalOutput").ap()
    build(nc, *args, out)
    r = _run(nc, [arrays], core_ids=[0])
    return r.results[0]["out_0"]
```

```python
from contextlib import ExitStack

import concourse.bass as bass
from concourse import mybir

F32 = mybir.dt.float32
F32R = mybir.dt.float32r
U32 = mybir.dt.uint32
ALU = mybir.AluOpType
ACT = mybir.ActivationFunctionType
AX = mybir.AxisListType

EPS = 1e-5


def wait(eng, sem, count):
    if not isinstance(count, int) or count > 0:
        eng.wait_ge(sem, count)


UNIT_BANKS = 3
PROLOGUE = ["c0", "c1", "k0", "k1", "k2", "k3", "v0", "xt0", "xt1", "v1", "q0", "v2"]
EVEN = [([], ["c0", "c1"]), ([], ["q1"]), (["k0", "k1"], []), ([], ["v2"]),
        ([], ["k2"]), ([], ["v0"]), (["xt0"], ["k3"]), (["wout", "xt1"], ["v1"])]
ODD = [(["c0"], ["c1"]), ([], []), (["k0"], []), ([], ["k2"]),
       (["v0"], ["k3"]), ([], ["wout", "q0"]), ([], []), (["v1", "k1", "v2"], [])]


def slots_of(p, odd, last):
    full = ODD if odd else EVEN
    drop = set()
    if not odd and isinstance(p, int) and p == 0:
        drop.add("wout")
    if last and odd:
        return [([], []), (["t0"], []), (["t1"], []), ([], []), ([], []), ([], ["wout"]), ([], []), ([], [])]
    if last:
        drop |= {"xt0", "xt1"}
    return [tuple([u for u in part if u not in drop] for part in slot) for slot in full]


def names_of(p, odd, last):
    return [u for early, late in slots_of(p, odd, last) for u in early + late]


def first_unit(p, odd, last):
    if isinstance(p, int) and p == 0:
        units, split = len(PROLOGUE), len(PROLOGUE)
    else:
        before = len(PROLOGUE) - 1
        units, split = before + 24 * p, before + 1 + 22 * p
    if odd:
        names = names_of(p, False, last)
        units, split = units + len(names), split + sum(u != "wout" for u in names)
    return units, split


def unit_count(p, odd, last, name):
    return first_unit(p, odd, last)[0] + names_of(p, odd, last).index(name) + 1


def split_count(p, odd, last, name):
    names = names_of(p, odd, last)
    return first_unit(p, odd, last)[1] + sum(u != "wout" for u in names[: names.index(name)]) + 1


def bank_of(p, odd, last, name):
    q = p if isinstance(p, int) else 1
    return (unit_count(q, odd, last, name) - 1) % UNIT_BANKS


def kv_count(p, odd, last, name):
    if odd or name == "q1":
        return unit_count(p, False, last, name)
    if isinstance(p, int) and p == 0:
        return PROLOGUE.index(name) + 1
    return unit_count(p - 1, True, False, name)


def build(nc, x, ctx, Wq, Wk, Wv, Wout, bout, Wr, rb, W1, W2, W3, Ws1, Ws2, Ws3, out):
    B, N, D = x.shape
    _, M, C = ctx.shape
    INNER = Wq.shape[1]
    HEADS, DH = 8, INNER // 8
    E, _, H = W1.shape
    TOKENS = B * N
    KR = 125
    KT = M // KR
    ME = M + 1
    CT = C - 128
    PAIRS = B // 2
    N2 = 2 * N
    assert KT * KR == M and CT == 64 and DH == 64 and D == 256 and B % 2 == 0
    QSCALE = DH ** -0.5
    RSCALE = D ** -0.5
    TILES = TOKENS // 128
    CHUNK = 512
    CHUNKS = TOKENS // CHUNK
    TC = CHUNK // 128
    MH = H // 128
    PIECES = 6
    assert CHUNKS == 7 and TILES == 28 and MH == 4

    xf = x.rearrange("b n d -> (b n) d")
    outf = out.rearrange("b n d -> (b n) d")
    x1_dram = nc.dram_tensor("x1_scratch", (TOKENS, D), F32, kind="Internal").ap()

    top = ExitStack()
    sb = lambda name, shape, dt=F32, at=top: at.enter_context(nc.sbuf_tensor(name, shape, dt))
    sem = lambda name: top.enter_context(nc.semaphore(name))

    with top:
        stage = sb("stage", [128, 4096])
        w_hi1 = sb("w_hi1", [128, PIECES * 512], F32R)
        w_lo1 = sb("w_lo1", [128, PIECES * 512], F32R)
        ident = sb("ident", [128, 128])
        x1 = [sb(f"x1_{i}", [N, D]) for i in range(2)]
        x1_first = sb("x1_first", [128, TC, D])
        xn2 = sb("xn2", [128, TC, D])
        stats2, mean_var2 = sb("stats2", [128, TC, 6]), sb("mean_var2", [128, TC, 2])
        var_eps2, rstd2 = sb("var_eps2", [128, TC]), sb("rstd2", [128, TC])
        minus_half2, eps2 = sb("minus_half2", [128, TC]), sb("eps2", [128, TC])
        firstT_hi, firstT_lo = sb("firstT_hi", [128, 2, CHUNK], F32R), sb("firstT_lo", [128, 2, CHUNK], F32R)
        wr, rb_sb = sb("wr", [128, 2, E]), sb("rb_sb", [128, E])
        wr_hi, wr_lo = sb("wr_hi", [128, 2, E], F32R), sb("wr_lo", [128, 2, E], F32R)
        bank = [top.enter_context(nc.psum_tensor(f"bank{i}", [128, 512], F32)) for i in range(8)]

        weights_in = [None, sem("weights_in1"), sem("weights_in2")]
        bout_in = sem("bout_in")
        x1_stored = [sem("x1_stored0"), sem("x1_stored1")]
        router_in = sem("router_in")
        sw_hi, sw_lo = sem("sw_hi"), sem("sw_lo")

        def load_expert(eng, w1, w3, w2, s):
            eng.dma_start(stage[:, 0:1024].rearrange("p (k n) -> p k n", k=2),
                          w1.rearrange("(k p) n -> p k n", p=128)).then_inc(s, 16)
            eng.dma_start(stage[:, 1024:2048].rearrange("p (k n) -> p k n", k=2),
                          w3.rearrange("(k p) n -> p k n", p=128)).then_inc(s, 16)
            eng.dma_start(stage[:, 2048:3072].rearrange("p (k n) -> p k n", k=4),
                          w2.rearrange("(k p) n -> p k n", p=128)).then_inc(s, 16)

        attention(nc, locals())
        experts(nc, locals())


def attention(nc, g):
    (x, ctx, Wq, Wk, Wv, Wout, bout, Ws1, Ws2, Ws3) = (g[k] for k in "x ctx Wq Wk Wv Wout bout Ws1 Ws2 Ws3".split())
    (N, D, M, ME, INNER, HEADS, DH, KR, KT, CT, PAIRS, N2, QSCALE) = (
        g[k] for k in "N D M ME INNER HEADS DH KR KT CT PAIRS N2 QSCALE".split())
    (stage, w_hi1, w_lo1, ident, bank, weights_in, bout_in, x1, x1_stored, sw_hi, sw_lo, x1_dram, load_expert) = (
        g[k] for k in "stage w_hi1 w_lo1 ident bank weights_in bout_in x1 x1_stored sw_hi sw_lo x1_dram load_expert".split())
    (x1_first, xn2, stats2, mean_var2, var_eps2, rstd2, minus_half2, eps2, firstT_hi, firstT_lo) = (
        g[k] for k in "x1_first xn2 stats2 mean_var2 var_eps2 rstd2 minus_half2 eps2 firstT_hi firstT_lo".split())
    (wr, rb_sb, wr_hi, wr_lo, router_in, W1, W2, W3, Wr, rb, PIECES, TC, CHUNK, E) = (
        g[k] for k in "wr rb_sb wr_hi wr_lo router_in W1 W2 W3 Wr rb PIECES TC CHUNK E".split())

    own = ExitStack()
    sb = lambda name, shape, dt=F32: own.enter_context(nc.sbuf_tensor(name, shape, dt))
    sem = lambda name: own.enter_context(nc.semaphore(name))
    with own:
        wq_hi, wq_lo = sb("wq_hi", [128, 2, INNER], F32R), sb("wq_lo", [128, 2, INNER], F32R)
        wk_hi, wk_lo = sb("wk_hi", [128, 2, INNER], F32R), sb("wk_lo", [128, 2, INNER], F32R)
        wv_hi, wv_lo = sb("wv_hi", [128, 2, INNER], F32R), sb("wv_lo", [128, 2, INNER], F32R)
        wo_hi, wo_lo = sb("wo_hi", [128, 4, D], F32R), sb("wo_lo", [128, 4, D], F32R)
        bout_sb = sb("bout_sb", [N, D])

        x_in = sb("x_in", [N, 2, D])
        xn = sb("xn", [N, 2, D])
        stats = sb("stats", [N, 2, 6])
        mean_var = sb("mean_var", [N, 2, 2])
        var_eps = sb("var_eps", [N, 2])
        minus_half, eps = sb("minus_half", [N, 2]), sb("eps", [N, 2])
        rstd = sb("rstd", [N, 2])
        xT_hi, xT_lo = sb("xT_hi", [128, 2, N2], F32R), sb("xT_lo", [128, 2, N2], F32R)
        ctx_in = [sb(f"ctx_in{i}", [KR, KT, 256]) for i in range(2)]
        cT_hi, cT_lo = sb("cT_hi", [128, ME], F32R), sb("cT_lo", [128, ME], F32R)
        cT_tail = sb("cT_tail", [128, ME], F32R)
        q_hi, q_lo = sb("q_hi", [128, HEADS, 2, N], F32R), sb("q_lo", [128, HEADS, 2, N], F32R)
        k_hi = [sb(f"k_hi{i}", [128, 4, ME], F32R) for i in range(2)]
        k_lo = [sb(f"k_lo{i}", [128, 4, ME], F32R) for i in range(2)]
        v_hi = [sb(f"v_hi{i}", [KR, KT, INNER], F32R) for i in range(2)]
        v_lo = [sb(f"v_lo{i}", [KR, KT, INNER], F32R) for i in range(2)]
        probs = sb("probs", [N, 4, M])
        neg_max, row_sum, inv_sum = sb("neg_max", [N, 16]), sb("row_sum", [N, 16]), sb("inv_sum", [N, 16])
        pT_hi = sb("pT_hi", [KR, 2, KT, 2, N], F32R)
        pT_lo = sb("pT_lo", [KR, 2, KT, 2, N], F32R)
        oT_hi = [sb(f"oT_hi{i}", [128, 4, N], F32R) for i in range(2)]
        oT_lo = [sb(f"oT_lo{i}", [128, 4, N], F32R) for i in range(2)]
        x_res = [sb(f"x_res{i}", [N, D]) for i in range(2)]
        S_BANK, PT_BANK, O_BANK, U_BANK = bank[0:2], bank[2:4], bank[4], bank[5:8]

        x_loaded = sem("x_loaded")
        ctx_loaded = [sem("ctx_loaded0"), sem("ctx_loaded1")]
        res_loaded = [sem("res_loaded0"), sem("res_loaded1")]
        norm_consts, ident_zero = sem("norm_consts"), sem("ident_zero")
        zeros_ready, q_zeros = sem("zeros_ready"), sem("q_zeros")
        ident_ready = sem("ident_ready")
        aw_in = {kind: sem(f"aw_in_{kind}") for kind in "kvqo"}
        aw_hi = sem("aw_hi")
        aw_lo = {kind: sem(f"aw_lo_{kind}") for kind in "kvqo"}
        stats_done, var_ready, var_eps_ready, rstd_ready, xn_ready = (
            sem(n) for n in "stats_done var_ready var_eps_ready rstd_ready xn_ready".split())
        unit_made, unit_hi, unit_done = sem("unit_made"), sem("unit_hi"), sem("unit_done")
        res_biased = sem("res_biased")
        scores_made, max_ready, exp_ready, inv_ready, probs_ready = (
            sem(n) for n in "scores_made max_ready exp_ready inv_ready probs_ready".split())
        first_loaded, first_stats, first_var, first_var_eps, first_rstd, first_normed = (
            sem("first_" + n) for n in "loaded stats var var_eps rstd normed".split())
        norm_consts2, wr_hi_ready, wr_ready = sem("norm_consts2"), sem("wr_hi_ready"), sem("wr_ready")
        pT_made, pT_hi_ready, pT_ready = sem("pT_made"), sem("pT_hi_ready"), sem("pT_ready")
        o_made, o_hi_ready, o_ready = sem("o_made"), sem("o_hi_ready"), sem("o_ready")

        AW = [("k", 0), ("k", 1), ("v", 0), ("v", 1), ("q", 0), ("q", 1), ("o", 0), ("o", 1)]
        AW_LOADS = {"k": 48, "v": 48, "q": 32, "o": 16}
        HI = {"q": wq_hi, "k": wk_hi, "v": wv_hi, "o": wo_hi}
        LO = {"q": wq_lo, "k": wk_lo, "v": wv_lo, "o": wo_lo}

        def piece(t, kind, i):
            return t[:, 2 * i:2 * i + 2, :] if kind == "o" else t[:, i, :]

        def staged(n, kind):
            s = stage[:, n * 512:(n + 1) * 512]
            return s.rearrange("p (k n) -> p k n", k=2) if kind == "o" else s

        def split_lo(eng, n):
            kind, i = AW[n]
            eng.wait_ge(aw_hi, n + 1)
            rows = slice(0, 64) if kind in "kv" and i == 1 else slice(0, 128)
            lo, hi, w = piece(LO[kind], kind, i)[rows], piece(HI[kind], kind, i)[rows].bitcast(F32), staged(n, kind)[rows]
            if kind == "q":
                eng.scalar_tensor_tensor(lo, w, QSCALE, hi, ALU.mult, ALU.subtract).then_inc(aw_lo[kind], 1)
            else:
                eng.tensor_tensor(lo, w, hi, ALU.subtract).then_inc(aw_lo[kind], 1)

        def heads_of(name, half):
            first = 4 * int(name[1]) + half
            return slice(first, first + 3, 2)

        def ps_q(ps, rows):
            return ps[rows, 0:2 * N2].rearrange("p (m b n) -> p m b n", m=2, b=2)

        def rounds(eng, body):
            body(0, False)
            with eng.Fori(1, PAIRS - 1) as p:
                body(p, False)
            body(PAIRS - 1, True)

        def ctx_rows(b):
            return ctx[bass.ds(b, 1), :, :].rearrange("o (t r) c -> r (o t) c", r=KR)

        def batch_of(b):
            return x[bass.ds(b, 1), :, :].rearrange("o r d -> (o r) d")

        def x_rows(b, n):
            return x[bass.ds(b, n), :, :].rearrange("b r d -> r b d")

        block = own.enter_context(nc.Block())

        @block.sync
        def _(sp):
            def load_ctx(b, i):
                rows = ctx_rows(b)
                sp.dma_start(ctx_in[i][:, :, 0:192], rows).then_inc(ctx_loaded[i], 16)
                sp.dma_start(ctx_in[i][:, :, 192:256], rows[:, :, 128:192]).then_inc(ctx_loaded[i], 16)

            def load_weight(w, n, kind, split_rows):
                sp.dma_start(stage[:, n * 512:(n + 1) * 512], w[0:128, :]).then_inc(aw_in[kind], 16)
                if split_rows:
                    sp.dma_start(stage[0:64, (n + 1) * 512:(n + 2) * 512], w[128:192, :]).then_inc(aw_in[kind], 16)
                    sp.dma_start(stage[64:128, (n + 1) * 512:(n + 2) * 512], w[128:192, :]).then_inc(aw_in[kind], 16)
                else:
                    sp.dma_start(stage[:, (n + 1) * 512:(n + 2) * 512], w[128:256, :]).then_inc(aw_in[kind], 16)

            load_ctx(0, 0)
            sp.dma_start(x_in[:], x_rows(0, 2)).then_inc(x_loaded, 16)
            load_weight(Wk, 0, "k", True)
            load_weight(Wv, 2, "v", True)
            load_weight(Wq, 4, "q", False)
            sp.dma_start(stage[:, 3072:4096].rearrange("p (k n) -> p k n", k=4),
                         Wout.rearrange("(k p) n -> p k n", p=128)).then_inc(aw_in["o"], 16)
            sp.dma_start(bout_sb[:], bout.rearrange("(o d) -> o d", o=1).to_broadcast([N, D])).then_inc(bout_in, 16)
            load_ctx(1, 1)
            sp.dma_start(wr[:], Wr.rearrange("(k p) e -> p k e", p=128)).then_inc(router_in, 16)
            sp.dma_start(rb_sb[:], rb.rearrange("(o e) -> o e", o=1).to_broadcast([128, E])).then_inc(router_in, 16)
            sp.dma_start(x_res[0][:], x[0]).then_inc(res_loaded[0], 16)
            sp.dma_start(x_res[1][:], x[1]).then_inc(res_loaded[1], 16)
            sp.wait_ge(xn_ready, 1)
            sp.dma_start(x_in[:], x_rows(2, 2)).then_inc(x_loaded, 16)
            sp.wait_ge(unit_made, PROLOGUE.index("c1") + 1)
            load_ctx(2, 0)
            sp.wait_ge(aw_hi, len(AW))
            for kind in "kvqo":
                sp.wait_ge(aw_lo[kind], 2)
            load_expert(sp, Ws1, Ws3, Ws2, weights_in[1])

            def store(b, i, count):
                sp.wait_ge(unit_done, count)
                sp.dma_start(x1_dram[bass.ds(b * N, N), :], x1[i][:]).then_inc(x1_stored[i], 16)

            def body(p, last):
                first = isinstance(p, int) and p == 0
                two_more = not isinstance(p, int) or p + 2 < PAIRS
                if not last:
                    sp.wait_ge(unit_made, unit_count(p, False, last, "c1"))
                    load_ctx(2 * p + 3, 1)
                if not first:
                    store(2 * p - 1, 1, unit_count(p, False, last, "wout"))
                    sp.dma_start(x_res[1][:], batch_of(2 * p + 1)).then_inc(res_loaded[1], 16)
                if two_more:
                    sp.wait_ge(xn_ready, p + 2)
                    sp.dma_start(x_in[:], x_rows(2 * p + 4, 2)).then_inc(x_loaded, 16)
                    sp.wait_ge(unit_made, unit_count(p, True, last, "c1"))
                    load_ctx(2 * p + 4, 0)
                store(2 * p, 0, unit_count(p, True, last, "wout"))
                if not last:
                    sp.dma_start(x_res[0][:], batch_of(2 * p + 2)).then_inc(res_loaded[0], 16)

            body(0, False)
            with sp.Fori(1, PAIRS - 2) as p:
                body(p, False)
            body(PAIRS - 2, False)
            for i in range(2):
                sp.wait_ge(x1_stored[i], 16 * (PAIRS - 2 + i))
            sp.dma_start(x1_first[:], x1_dram[0:CHUNK, :].rearrange("(t p) d -> p t d", p=128)).then_inc(first_loaded, 16)
            body(PAIRS - 1, True)
            sp.wait_ge(unit_done, unit_count(PAIRS - 1, True, True, "wout") + 1)
            sp.dma_start(x1_dram[(2 * PAIRS - 1) * N:2 * PAIRS * N, :], x1[1][:]).then_inc(x1_stored[1], 16)
            sp.wait_ge(sw_hi, PIECES)
            sp.wait_ge(sw_lo, PIECES)
            load_expert(sp, W1[0], W3[0], W2[0], weights_in[2])

        @block.gpsimd
        def _(pool):
            pool.memset(ident[:], 0.0).then_inc(ident_zero, 1)
            pool.memset(minus_half[:], -0.5).then_inc(norm_consts, 1)
            pool.memset(eps[:], EPS).then_inc(norm_consts, 1)
            pool.memset(minus_half2[:], -0.5).then_inc(norm_consts2, 1)
            pool.memset(eps2[:], EPS).then_inc(norm_consts2, 1)
            pool.wait_ge(ident_zero, 1)
            pool.affine_select(out=ident[:], in_=ident[:], compare_op=ALU.not_equal, fill=1.0, base=0,
                               pattern=[[-1, 128]], channel_multiplier=1).then_inc(ident_ready, 1)

            def rstd_of(n):
                pool.wait_ge(var_ready, n)
                pool.tensor_tensor(var_eps[:], mean_var[:, :, 1], eps[:], ALU.add).then_inc(var_eps_ready, 1)
                pool.wait_ge(var_eps_ready, n)
                pool.tensor_tensor(rstd[:], var_eps[:], minus_half[:], ALU.pow).then_inc(rstd_ready, 1)

            def add_bout(i, n):
                pool.wait_ge(res_loaded[i], 16 * n)
                pool.tensor_tensor(x_res[i][:], x_res[i][:], bout_sb[:], ALU.add).then_inc(res_biased, 1)

            pool.wait_ge(norm_consts, 2)
            rstd_of(1)
            for n in (2, 3):
                split_lo(pool, n)
            for n in (6, 7):
                split_lo(pool, n)
            pool.wait_ge(bout_in, 16)
            add_bout(0, 1)
            add_bout(1, 1)

            def body(p, last):
                for s in range(16):
                    pool.wait_ge(inv_ready, 16 * p + s + 1)
                    pool.tensor_tensor(probs[:, s % 4, :], probs[:, s % 4, :],
                                       inv_sum[:, s:s + 1].to_broadcast([N, M]), ALU.mult).then_inc(probs_ready, 1)
                    if s == 2 and not last:
                        rstd_of(p + 2)
                    if s == 5 and last:
                        pool.wait_ge(norm_consts2, 2)
                        pool.wait_ge(first_var, 1)
                        pool.tensor_tensor(var_eps2[:], mean_var2[:, :, 1], eps2[:], ALU.add).then_inc(first_var_eps, 1)
                        pool.wait_ge(first_var_eps, 1)
                        pool.tensor_tensor(rstd2[:], var_eps2[:], minus_half2[:], ALU.pow).then_inc(first_rstd, 1)
                    if s in (1, 9) and not (isinstance(p, int) and p == 0):
                        add_bout(s // 8, p + 1)
                if isinstance(p, int) and p == 0:
                    pool.wait_ge(weights_in[1], 48)
                    for j in range(PIECES):
                        cols = slice(j * 512, (j + 1) * 512)
                        pool.wait_ge(sw_hi, j + 1)
                        pool.tensor_tensor(w_lo1[:, cols], stage[:, cols], w_hi1[:, cols].bitcast(F32),
                                           ALU.subtract).then_inc(sw_lo, 1)

            rounds(pool, body)

        @block.scalar
        def _(act):
            def split_hi(n):
                kind, i = AW[n]
                act.wait_ge(aw_in[kind], AW_LOADS[kind])
                act.activation(piece(HI[kind], kind, i), staged(n, kind), ACT.Copy,
                               scale=QSCALE if kind == "q" else 1.0).then_inc(aw_hi, 1)

            def unit(n_made, name, b, ps):
                act.wait_ge(unit_made, n_made)
                if name[0] == "x":
                    j = int(name[2])
                    act.activation(xT_hi[:, :, j * N:(j + 1) * N],
                                   ps[:, 0:2 * N].rearrange("p (k n) -> p k n", k=2), ACT.Copy).then_inc(unit_hi, 1)
                elif name[0] == "t":
                    act.activation(firstT_hi[:, int(name[1]), :], ps[:], ACT.Copy).then_inc(unit_hi, 1)
                elif name == "c0":
                    act.activation(cT_hi[:, 0:M], ps[:, 0:M], ACT.Copy).then_inc(unit_hi, 1)
                elif name == "c1":
                    act.activation(cT_tail[:, 0:M], ps[:, 0:M], ACT.Copy).then_inc(unit_hi, 1)
                elif name[0] == "q":
                    for half in range(2):
                        rows, heads = slice(64 * half, 64 * half + 64), heads_of(name, half)
                        last = act.activation(q_hi[rows, heads, :, :], ps_q(ps, rows), ACT.Copy)
                    last.then_inc(unit_hi, 1)
                elif name[0] == "k":
                    act.activation(k_hi[b][:, int(name[1]), :], ps[:, 0:ME], ACT.Copy).then_inc(unit_hi, 1)
                elif name[0] == "v":
                    act.activation(v_hi[b][:, int(name[1]), :], ps[0:KR, :], ACT.Copy).then_inc(unit_hi, 1)

            for n, name in enumerate(PROLOGUE):
                for i in {"k0": range(6), "k1": (6, 7)}.get(name, ()):
                    split_hi(i)
                unit(n + 1, name, 0, U_BANK[n % UNIT_BANKS])

            def o_part(a, j):
                act.wait_ge(o_made, a + 1)
                bk = O_BANK
                act.activation(oT_hi[j // 4][0:64, j % 4, :], bk[0:64, 0:N], ACT.Copy)
                act.activation(oT_hi[j // 4][64:128, j % 4, :], bk[64:128, N:N2], ACT.Copy).then_inc(o_hi_ready, 1)

            def slot(p, last, s, lead):
                gh = 16 * p + s
                odd = s // 8
                first = isinstance(p, int) and p == 0
                if lead:
                    act.wait_ge(max_ready, gh + 1)
                    wait(act, pT_made, gh - 3)
                    act.activation(probs[:, s % 4, :], S_BANK[s % 2][0:N, 0:M], ACT.Exp, bias=neg_max[:, s:s + 1],
                                   accum_out=row_sum[:, s:s + 1]).then_inc(exp_ready, 1)
                early, late = slots_of(p, bool(odd), last)[s % 8] if lead else ([], [])

                def run(names):
                    for name in names:
                        if name != "wout":
                            unit(unit_count(p, bool(odd), last, name), name, 1 - odd,
                                 U_BANK[bank_of(p, bool(odd), last, name)])

                run(early)
                if not (first and s < 2) and s < 18:
                    t = s - 2
                    act.wait_ge(pT_made, gh - 1)
                    wait(act, o_made, 8 * p + t // 2 - 1)
                    act.activation(pT_hi[:, (t // 2) % 2, :, t % 2, :],
                                   PT_BANK[t % 2][0:KR, 0:KT * N].rearrange("p (t n) -> p t n", t=KT),
                                   ACT.Copy).then_inc(pT_hi_ready, 1)
                run(late)
                if s % 2 == 0 and not (first and s < 4):
                    o_part(8 * p + s // 2 - 2, (s // 2 - 2) % 8)

            def body(p, last):
                for s in range(16):
                    slot(p, last, s, True)
                if isinstance(p, int) and p == 0:
                    act.wait_ge(weights_in[1], 48)
                    for j in range(PIECES):
                        cols = slice(j * 512, (j + 1) * 512)
                        act.activation(w_hi1[:, cols], stage[:, cols], ACT.Copy).then_inc(sw_hi, 1)
                    act.wait_ge(router_in, 32)
                    act.activation(wr_hi[:], wr[:], ACT.Copy).then_inc(wr_hi_ready, 1)

            rounds(act, body)
            for s in range(16, 19):
                slot(PAIRS - 1, True, s, False)

        @block.vector
        def _(dve):
            def statistics(n):
                dve.wait_ge(x_loaded, 16 * n)
                dve.bn_stats(stats[:, 0, :], x_in[:, 0, :])
                dve.bn_stats(stats[:, 1, :], x_in[:, 1, :]).then_inc(stats_done, 1)
                dve.wait_ge(x_loaded, 16)
                dve.wait_ge(stats_done, n)
                dve.bn_aggr(mean_var[:, 0, :], stats[:, 0, :])
                dve.bn_aggr(mean_var[:, 1, :], stats[:, 1, :]).then_inc(var_ready, 1)

            def normed(n):
                dve.wait_ge(rstd_ready, n)
                dve.wait_ge(var_ready, n)
                for j in range(2):
                    last = dve.tensor_scalar(xn[:, j, :], x_in[:, j, :], mean_var[:, j, 0:1], rstd[:, j:j + 1],
                                             ALU.subtract, ALU.mult)
                last.then_inc(xn_ready, 1)

            def first_statistics():
                dve.wait_ge(first_loaded, 16)
                for t in range(TC):
                    last = dve.bn_stats(stats2[:, t, :], x1_first[:, t, :])
                last.then_inc(first_stats, 1)
                dve.wait_ge(first_stats, 1)
                for t in range(TC):
                    last = dve.bn_aggr(mean_var2[:, t, :], stats2[:, t, :])
                last.then_inc(first_var, 1)

            def unit(n_hi, name, b, ps):
                dve.wait_ge(unit_hi, n_hi)
                if name[0] == "x":
                    cols = slice(int(name[2]) * N, (int(name[2]) + 1) * N)
                    dve.tensor_tensor(xT_lo[:, :, cols], ps[:, 0:2 * N].rearrange("p (k n) -> p k n", k=2),
                                      xT_hi[:, :, cols].bitcast(F32), ALU.subtract).then_inc(unit_done, 1)
                elif name[0] == "t":
                    dve.tensor_tensor(firstT_lo[:, int(name[1]), :], ps[:], firstT_hi[:, int(name[1]), :].bitcast(F32),
                                      ALU.subtract).then_inc(unit_done, 1)
                elif name == "c0":
                    dve.tensor_tensor(cT_lo[:, 0:M], ps[:, 0:M], cT_hi[:, 0:M].bitcast(F32), ALU.subtract).then_inc(unit_done, 1)
                elif name == "c1":
                    dve.tensor_tensor(cT_tail[64:128, 0:M], ps[64:128, 0:M], cT_tail[64:128, 0:M].bitcast(F32),
                                      ALU.subtract).then_inc(unit_done, 1)
                elif name[0] == "q":
                    for half in range(2):
                        rows, heads = slice(64 * half, 64 * half + 64), heads_of(name, half)
                        last = dve.tensor_tensor(q_lo[rows, heads, :, :], ps_q(ps, rows),
                                                 q_hi[rows, heads, :, :].bitcast(F32), ALU.subtract)
                    last.then_inc(unit_done, 1)
                elif name[0] == "k":
                    m = int(name[1])
                    dve.tensor_tensor(k_lo[b][:, m, :], ps[:, 0:ME], k_hi[b][:, m, :].bitcast(F32),
                                      ALU.subtract).then_inc(unit_done, 1)
                elif name[0] == "v":
                    t = int(name[1])
                    dve.tensor_tensor(v_lo[b][:, t, :], ps[0:KR, :], v_hi[b][:, t, :].bitcast(F32),
                                      ALU.subtract).then_inc(unit_done, 1)

            def residual(count, i, n_res, n_store, ps):
                dve.wait_ge(unit_made, count)
                dve.wait_ge(res_biased, n_res)
                wait(dve, x1_stored[i], 16 * (n_store + i))
                dve.tensor_tensor(x1[i][:], ps[0:N, 0:D], x_res[i][:], ALU.add).then_inc(unit_done, 1)

            def zero_heads(t):
                for half in range(2):
                    dve.memset(t[64 * half:64 * half + 64, :, :, :].rearrange(
                        "p (m e) b n -> p m e (b n)", e=2)[:, :, 1 - half, :].bitcast(F32), 0.0).then_inc(q_zeros, 1)

            for t in (wk_lo, wv_lo):
                dve.memset(t[64:128, 1, :].bitcast(F32), 0.0).then_inc(zeros_ready, 1)
            for t in (cT_hi, cT_lo, cT_tail):
                dve.memset(t[:, M:ME].bitcast(F32), 0.0).then_inc(zeros_ready, 1)
            dve.memset(x1[1][:], 0.0).then_inc(x1_stored[1], 16)
            zero_heads(q_hi)
            statistics(1)
            for n, name in enumerate(PROLOGUE):
                if name == "k0":
                    normed(1)
                    for i in (0, 1, 4, 5):
                        split_lo(dve, i)
                if name == "k1":
                    zero_heads(q_lo)
                unit(n + 1, name, 0, U_BANK[n % UNIT_BANKS])

            def run(p, odd, last, name):
                ps = U_BANK[bank_of(p, odd, last, name)]
                if name == "wout":
                    residual(unit_count(p, odd, last, name), 0 if odd else 1,
                             2 * p + 1 if odd else 2 * p, p if odd else p - 1, ps)
                else:
                    unit(split_count(p, odd, last, name), name, 0 if odd else 1, ps)

            def slot(p, last, s, lead):
                gh = 16 * p + s
                odd = bool(s // 8)
                first = isinstance(p, int) and p == 0
                if lead:
                    dve.wait_ge(scores_made, gh + 1)
                    dve.tensor_reduce(neg_max[:, s:s + 1], S_BANK[s % 2][0:N, 0:M], AX.X, ALU.max,
                                      negate=True).then_inc(max_ready, 1)
                if s == 0 and not first:
                    for name in ODD[7][1]:
                        run(p - 1, True, False, name)
                elif 0 < s <= 16 and not (last and s == 16):
                    was_odd = (s - 1) // 8 == 1
                    for name in slots_of(p, was_odd, last)[(s - 1) % 8][1]:
                        run(p, was_odd, last, name)
                if lead:
                    dve.wait_ge(exp_ready, gh + 1)
                    dve.reciprocal(inv_sum[:, s:s + 1], row_sum[:, s:s + 1]).then_inc(inv_ready, 1)
                if s % 2 == 1 and not (first and s < 5):
                    j = ((s - 1) // 2 - 2) % 8
                    dve.wait_ge(o_hi_ready, 8 * p + (s - 1) // 2 - 1)
                    dve.tensor_tensor(oT_lo[j // 4][0:64, j % 4, :], O_BANK[0:64, 0:N],
                                      oT_hi[j // 4][0:64, j % 4, :].bitcast(F32), ALU.subtract)
                    dve.tensor_tensor(oT_lo[j // 4][64:128, j % 4, :], O_BANK[64:128, N:N2],
                                      oT_hi[j // 4][64:128, j % 4, :].bitcast(F32), ALU.subtract).then_inc(o_ready, 1)
                for name in slots_of(p, odd, last)[s % 8][0] if lead else []:
                    run(p, odd, last, name)
                if not (first and s < 2) and s < 18:
                    t = s - 2
                    dve.wait_ge(pT_hi_ready, gh - 1)
                    dve.tensor_tensor(pT_lo[:, (t // 2) % 2, :, t % 2, :],
                                      PT_BANK[t % 2][0:KR, 0:KT * N].rearrange("p (t n) -> p t n", t=KT),
                                      pT_hi[:, (t // 2) % 2, :, t % 2, :].bitcast(F32),
                                      ALU.subtract).then_inc(pT_ready, 1)
                if s == 1 and lead and not last:
                    statistics(p + 2)
                if s == 4 and lead and not last:
                    normed(p + 2)
                if s == 3 and last:
                    first_statistics()
                if s == 7 and last:
                    dve.wait_ge(first_rstd, 1)
                    for t in range(TC):
                        mm = dve.tensor_scalar(xn2[:, t, :], x1_first[:, t, :], mean_var2[:, t, 0:1],
                                               rstd2[:, t:t + 1], ALU.subtract, ALU.mult)
                    mm.then_inc(first_normed, 1)
                if s == 12 and last:
                    dve.wait_ge(wr_hi_ready, 1)
                    dve.tensor_tensor(wr_lo[:], wr[:], wr_hi[:].bitcast(F32), ALU.subtract).then_inc(wr_ready, 1)

            def body(p, last):
                for s in range(16):
                    slot(p, last, s, True)

            rounds(dve, body)
            for s in range(16, 20):
                slot(PAIRS - 1, True, s, False)
            n = unit_count(PAIRS - 1, True, True, "wout") + 1
            residual(n, 1, 2 * PAIRS, PAIRS - 1, U_BANK[(n - 1) % UNIT_BANKS])

        @block.tensor
        def _(pe):
            def product(o, pairs):
                for n, (lhsT, rhs) in enumerate(pairs):
                    mm = pe.matmul(o, lhsT, rhs, start=(n == 0), stop=(n == len(pairs) - 1))
                return mm

            def unit(count, name, b, ps):
                wait(pe, unit_done, count - UNIT_BANKS)
                if name[0] == "x":
                    j = int(name[2])
                    for k in range(2):
                        mm = pe.transpose(ps[:, k * N:(k + 1) * N], xn[:, j, k * 128:(k + 1) * 128], ident[0:N, 0:N])
                elif name[0] == "t":
                    k = int(name[1])
                    for t in range(TC):
                        mm = pe.transpose(ps[:, t * 128:(t + 1) * 128], xn2[:, t, k * 128:(k + 1) * 128], ident[:])
                elif name[0] == "c":
                    c = int(name[1]) * 128
                    for t in range(KT):
                        mm = pe.transpose(ps[:, t * KR:(t + 1) * KR], ctx_in[b][:, t, c:c + 128], ident[0:KR, 0:KR])
                elif name[0] == "q":
                    for m in range(2):
                        cols = slice((2 * int(name[1]) + m) * 128, (2 * int(name[1]) + m + 1) * 128)
                        mm = product(ps[:, m * N2:(m + 1) * N2],
                                     [(w[:, k, cols], v[:, k, :]) for k in range(2)
                                      for w, v in ((wq_hi, xT_hi), (wq_hi, xT_lo), (wq_lo, xT_hi))])
                elif name[0] == "k":
                    cols = slice(int(name[1]) * 128, int(name[1]) * 128 + 128)
                    mm = product(ps[:, 0:ME], [(wk_hi[:, 0, cols], cT_hi[:]), (wk_hi[:, 0, cols], cT_lo[:]),
                                              (wk_lo[:, 0, cols], cT_hi[:]), (wk_hi[:, 1, cols], cT_tail[:]),
                                              (wk_lo[:, 1, cols], cT_tail[:])])
                elif name[0] == "v":
                    r = slice(int(name[1]) * KR, (int(name[1]) + 1) * KR)
                    mm = product(ps[0:KR, :], [(cT_hi[:, r], wv_hi[:, 0, :]), (cT_lo[:, r], wv_hi[:, 0, :]),
                                               (cT_hi[:, r], wv_lo[:, 0, :]), (cT_tail[:, r], wv_hi[:, 1, :]),
                                               (cT_tail[:, r], wv_lo[:, 1, :])])
                elif name == "wout":
                    mm = product(ps[0:N, 0:D], [(o[b][:, k, :], w[:, k, :]) for k in range(4)
                                                for o, w in ((oT_hi, wo_hi), (oT_lo, wo_hi), (oT_hi, wo_lo))])
                mm.then_inc(unit_made, 1)

            pe.wait_ge(ident_ready, 1)
            for n, name in enumerate(PROLOGUE):
                if name == "xt0":
                    pe.wait_ge(xn_ready, 1)
                if name == "c0":
                    pe.wait_ge(ctx_loaded[0], 32)
                if name == "k0":
                    pe.wait_ge(zeros_ready, 5)
                    pe.wait_ge(aw_lo["k"], 2)
                    pe.wait_ge(unit_done, n)
                if name == "v0":
                    pe.wait_ge(aw_lo["v"], 2)
                if name == "q0":
                    pe.wait_ge(aw_lo["q"], 2)
                    pe.wait_ge(unit_done, PROLOGUE.index("xt1") + 1)
                unit(n + 1, name, 0, U_BANK[n % UNIT_BANKS])
            pe.wait_ge(q_zeros, 4)

            def slot(p, last, s, lead):
                gh = 16 * p + s
                odd = bool(s // 8)
                first = isinstance(p, int) and p == 0
                h = s % 8
                if lead:
                    if s in (0, 4):
                        pe.wait_ge(unit_done, kv_count(p, False, last, f"q{s // 4}"))
                    pe.wait_ge(unit_done, kv_count(p, odd, last, f"k{h // 2}"))
                    wait(pe, exp_ready, gh - 1)
                    i, m = int(odd), h // 2
                    product(S_BANK[s % 2][0:N, 0:ME], [(q_hi[:, h, i, :], k_hi[i][:, m, :]),
                                                      (q_hi[:, h, i, :], k_lo[i][:, m, :]),
                                                      (q_lo[:, h, i, :], k_hi[i][:, m, :])]).then_inc(scores_made, 1)
                early, late = slots_of(p, odd, last)[h] if lead else ([], [])

                def run(name):
                    count = unit_count(p, odd, last, name)
                    if name == "xt0":
                        pe.wait_ge(xn_ready, p + 2)
                    if name == "c0":
                        pe.wait_ge(ctx_loaded[0 if odd else 1], 32 * (p + 2 if odd else p + 1))
                    if name == "k0":
                        pe.wait_ge(unit_done, unit_count(p, odd, last, "c1"))
                    if name == "q0":
                        pe.wait_ge(unit_done, unit_count(p, False, last, "xt1"))
                    if name == "t0":
                        pe.wait_ge(first_normed, 1)
                    if name == "wout" and first:
                        pe.wait_ge(aw_lo["o"], 2)
                    if name == "wout":
                        pe.wait_ge(o_ready, 8 * p + 4 if odd else 8 * p)
                    unit(count, name, 0 if odd else 1, U_BANK[bank_of(p, odd, last, name)])

                for name in early:
                    run(name)
                if not (first and s < 2) and s < 18:
                    t = s - 2
                    pe.wait_ge(probs_ready, gh - 1)
                    wait(pe, pT_ready, gh - 3)
                    for kt in range(KT):
                        mm = pe.transpose(PT_BANK[t % 2][0:KR, kt * N:(kt + 1) * N],
                                          probs[:, t % 4, kt * KR:(kt + 1) * KR], ident[0:N, 0:N])
                    mm.then_inc(pT_made, 1)
                for name in late:
                    run(name)
                if s % 2 == 0 and not (first and s < 4):
                    a = 8 * p + s // 2 - 2
                    j = (s // 2 - 2) % 8
                    i, m = j // 4, j % 4
                    pe.wait_ge(pT_ready, 2 * a + 2)
                    if m == 0:
                        pe.wait_ge(unit_done, kv_count(p, i == 1, last, "v2"))
                    wait(pe, o_ready, a)
                    vh, vl, cols = v_hi[i], v_lo[i], slice(m * 128, (m + 1) * 128)
                    pt = [t[:, j % 2, :, :, :].rearrange("p t e n -> p t (e n)") for t in (pT_hi, pT_lo)]
                    product(O_BANK[:, 0:N2],
                            [(v[:, kt, cols], w[:, kt, :]) for kt in range(KT)
                             for v, w in ((vh, pt[0]), (vh, pt[1]), (vl, pt[0]))]).then_inc(o_made, 1)

            def body(p, last):
                for s in range(16):
                    slot(p, last, s, True)

            rounds(pe, body)
            for s in range(16, 19):
                slot(PAIRS - 1, True, s, False)
            n = unit_count(PAIRS - 1, True, True, "wout") + 1
            pe.wait_ge(wr_ready, 1)
            pe.wait_ge(o_ready, 8 * PAIRS)
            unit(n, "wout", 1, U_BANK[(n - 1) % UNIT_BANKS])


def experts(nc, g):
    (W1, W2, W3, outf, x1_dram) = (g[k] for k in "W1 W2 W3 outf x1_dram".split())
    PAIRS, wr_hi, wr_lo, rb_sb, x1_first, x1_stored = (
        g[k] for k in "PAIRS wr_hi wr_lo rb_sb x1_first x1_stored".split())
    (xn, stats, mean_var, var_eps, rstd, minus_half, firstT_hi, firstT_lo) = (
        g[k] for k in "xn2 stats2 mean_var2 var_eps2 rstd2 minus_half2 firstT_hi firstT_lo".split())
    (D, E, H, TILES, CHUNK, CHUNKS, TC, MH, PIECES, RSCALE) = (
        g[k] for k in "D E H TILES CHUNK CHUNKS TC MH PIECES RSCALE".split())
    (stage, w_hi1, w_lo1, ident, bank, weights_in, load_expert) = (
        g[k] for k in "stage w_hi1 w_lo1 ident bank weights_in load_expert".split())

    own = ExitStack()
    sb = lambda name, shape, dt=F32: own.enter_context(nc.sbuf_tensor(name, shape, dt))
    sem = lambda name: own.enter_context(nc.semaphore(name))
    with own:
        w_hi = [sb("w_hi0", [128, PIECES * 512], F32R), w_hi1]
        w_lo = [sb("w_lo0", [128, PIECES * 512], F32R), w_lo1]
        acc = sb("acc", [128, TILES, D])
        REST = (CHUNKS - 1) * CHUNK
        xT_hi, xT_lo = sb("x2T_hi", [128, 2, REST], F32R), sb("x2T_lo", [128, 2, REST], F32R)
        hT_hi = [sb(f"hT_hi{i}", [128, MH, CHUNK], F32R) for i in range(2)]
        hT_lo = [sb(f"hT_lo{i}", [128, MH, CHUNK], F32R) for i in range(2)]
        tanh = x1_first[:].rearrange("p (m a) d -> p m (a d)", m=2)
        gate = sb("gate", [128, CHUNK])
        hidden = sb("hidden", [128, 2, CHUNK])
        logits = sb("logits", [128, TILES, E])
        biased = sb("biased", [128, TILES, E])
        top = sb("top", [128, TILES, 8])
        top_at = sb("top_at", [128, TILES, 8], U32)
        top_atf = sb("top_atf", [128, TILES, 2])
        iota = sb("iota", [128, E])
        pick = sb("pick", [128, 2, TILES, E])
        picked = sb("picked", [128, 2, TILES, E])
        chosen = sb("chosen", [128, 2, TILES])
        most, total, total_inv = sb("most", [128, TILES]), sb("total", [128, TILES]), sb("total_inv", [128, TILES])
        share = sb("share", [128, 1 + E, TILES])
        H_BANK, Y_BANK, X_BANK = (bank[0:2], bank[2:4]), bank[4:6], bank[6:8]

        x1_loaded = [sem(f"x1_loaded{c}") for c in range(CHUNKS)]
        consts = sem("consts2")
        stats_done, var_ready, var_eps_ready, rstd_ready, xn_ready = (
            sem(n + "2") for n in "stats_done var_ready var_eps_ready rstd_ready xn_ready".split())
        xT_made, xT_hi_ready, xT_ready = sem("xT_made"), sem("xT_hi_ready"), sem("xT_ready")
        logits_made, logits_ready = sem("logits_made"), sem("logits_ready")
        route = sem("route")
        chosen_ready, chosen_exp = sem("chosen_ready"), sem("chosen_exp")
        a3_made, a1_made = sem("a3_made"), sem("a1_made")
        tanh_ready, gate_ready, hidden_ready = sem("tanh_ready"), sem("gate_ready"), sem("hidden_ready")
        h_hi_ready, h_ready = sem("h_hi_ready"), sem("h_ready")
        y_made, y_added = sem("y_made"), sem("y_added")
        piece_hi, piece_lo = sem("piece_hi"), sem("piece_lo")
        out_stored = sem("out_stored")
        LAST_PAIR = E // 2 - 1

        def shared(step):
            for c in range(CHUNKS):
                step(c, c, 1, None, c, c > 0)

        def routed(eng, step, between=None):
            def pair(i, last):
                for odd in range(2):
                    n = CHUNKS + 2 * CHUNKS * i + CHUNKS * odd
                    e = 2 * i + odd
                    step(n, 0, odd, e, 0, True, last)
                    with eng.Fori(0, 3) as j:
                        for k in range(2):
                            step(n + 2 * j + 1 + k, 2 * j + 1 + k, odd, e, 1 + k, True, last)

            with eng.Fori(0, LAST_PAIR) as i:
                pair(i, False)
            pair(LAST_PAIR, True)

        def tokens(c):
            if isinstance(c, int) and c == 0:
                return firstT_hi, firstT_lo, slice(0, CHUNK)
            return xT_hi, xT_lo, bass.ds((c - 1) * CHUNK, CHUNK)

        block = own.enter_context(nc.Block())

        @block.sync
        def _(sp):
            x1_rows = x1_dram.rearrange("(t p) d -> p t d", p=128)
            for c in [1, 0] + list(range(2, CHUNKS)):
                if c == CHUNKS - 1:
                    for i in range(2):
                        sp.wait_ge(x1_stored[i], 16 * (PAIRS + i))
                sp.dma_start(acc[:, c * TC:(c + 1) * TC, :], x1_rows[:, c * TC:(c + 1) * TC, :]).then_inc(x1_loaded[c], 16)
            def fetch(e, n):
                sp.wait_ge(piece_hi, PIECES * n)
                sp.wait_ge(piece_lo, PIECES * n)
                load_expert(sp, *(w[bass.ds(e, 1), :, :].rearrange("o d h -> (o d) h") for w in (W1, W3, W2)),
                            weights_in[2])

            with sp.Fori(1, E) as e:
                fetch(e, e)
            out_rows = outf.rearrange("(t p) d -> p t d", p=128)
            for c in range(CHUNKS):
                sp.wait_ge(y_added, TILES * E + TC * (c + 1))
                sp.dma_start(out_rows[:, c * TC:(c + 1) * TC, :], acc[:, c * TC:(c + 1) * TC, :]).then_inc(out_stored, 16)
            sp.wait_ge(out_stored, 16 * CHUNKS)

        @block.gpsimd
        def _(pool):
            pool.iota(iota[:], pattern=[[1, E]], base=0, channel_multiplier=0,
                      allow_small_or_imprecise_dtypes=True).then_inc(consts, 1)
            pool.memset(share[:, 0, :], 1.0).then_inc(consts, 1)

            def rstd_of(c):
                pool.wait_ge(var_ready, c)
                pool.tensor_scalar(var_eps[:], mean_var[:, :, 1], EPS, 1.0, ALU.add, ALU.mult).then_inc(var_eps_ready, 1)
                pool.wait_ge(var_eps_ready, c)
                pool.tensor_tensor(rstd[:], var_eps[:], minus_half[:], ALU.pow).then_inc(rstd_ready, 1)

            def lo_of_hidden(n, s):
                for m in range(MH):
                    pool.wait_ge(h_hi_ready, MH * n + m + 1)
                    pool.tensor_tensor(hT_lo[s][:, m, :], hidden[:, m % 2, :], hT_hi[s][:, m, :].bitcast(F32),
                                       ALU.subtract).then_inc(h_ready, 1)

            def lo_of_piece(n, j, buf):
                pool.wait_ge(piece_hi, PIECES * n + j + 1)
                cols = bass.ds(j * 512, 512)
                pool.tensor_tensor(w_lo[buf][:, cols], stage[:, cols], w_hi[buf][:, cols].bitcast(F32),
                                   ALU.subtract).then_inc(piece_lo, 1)

            rstd_of(1)
            for c in range(CHUNKS):
                lo_of_hidden(c, c % 2)
                if c + 2 < CHUNKS:
                    rstd_of(c + 2)
                if c > 0:
                    lo_of_piece(0, c - 1, 0)

            def step(n, c, buf, e, k, prev, last):
                lo_of_hidden(n, (CHUNKS + CHUNKS * buf + k) % 2)
                if k > 0 and not (last and buf == 1):
                    lo_of_piece(e + 1, c - 1, 1 - buf)

            routed(pool, step)

        @block.scalar
        def _(act):
            def hi_of_x(c):
                hi, _, cols = tokens(c)
                for k in range(2):
                    act.wait_ge(xT_made, 2 * c + k - 1)
                    act.activation(hi[:, k, cols], X_BANK[k][:], ACT.Copy).then_inc(xT_hi_ready, 1)

            def chosen_exps():
                act.wait_ge(chosen_ready, 1)
                act.activation(chosen[:], chosen[:], ACT.Exp).then_inc(chosen_exp, 1)

            def units(n, s):
                for m in range(MH):
                    act.wait_ge(a3_made, MH * n + m + 1)
                    act.activation(tanh[:, m % 2, :], H_BANK[0][m % 2][:], ACT.Tanh, scale=0.5).then_inc(tanh_ready, 1)
                    act.wait_ge(hidden_ready, MH * n + m + 1)
                    act.activation(hT_hi[s][:, m, :], hidden[:, m % 2, :], ACT.Copy).then_inc(h_hi_ready, 1)
                    if isinstance(n, int) and n < CHUNKS - 1 and m == 2:
                        hi_of_x(n + 1)

            def hi_of_piece(n, j, buf):
                if not isinstance(j, int) or j == 0:
                    act.wait_ge(weights_in[2], 48 * (n + 1))
                cols = bass.ds(j * 512, 512)
                act.activation(w_hi[buf][:, cols], stage[:, cols], ACT.Copy).then_inc(piece_hi, 1)

            for c in range(CHUNKS):
                units(c, c % 2)
                if c + 1 == CHUNKS:
                    chosen_exps()
                if c > 0:
                    hi_of_piece(0, c - 1, 0)

            def step(n, c, buf, e, k, prev, last):
                units(n, (CHUNKS + CHUNKS * buf + k) % 2)
                if k > 0 and not (last and buf == 1):
                    if k == 1:
                        act.wait_ge(y_made, TILES * (e + 1))
                    hi_of_piece(e + 1, c - 1, 1 - buf)

            routed(act, step)

        @block.vector
        def _(dve):
            def statistics(c):
                dve.wait_ge(x1_loaded[c], 16)
                for t in range(TC):
                    last = dve.bn_stats(stats[:, t, :], acc[:, c * TC + t, :])
                last.then_inc(stats_done, 1)
                dve.wait_ge(stats_done, c)
                for t in range(TC):
                    last = dve.bn_aggr(mean_var[:, t, :], stats[:, t, :])
                last.then_inc(var_ready, 1)

            def normed(c):
                dve.wait_ge(rstd_ready, c)
                wait(dve, xT_made, 2 * (c - 1))
                for t in range(TC):
                    last = dve.tensor_scalar(xn[:, t, :], acc[:, c * TC + t, :], mean_var[:, t, 0:1],
                                             rstd[:, t:t + 1], ALU.subtract, ALU.mult)
                last.then_inc(xn_ready, 1)

            def lo_of_x(c, k):
                hi, lo, cols = tokens(c)
                dve.wait_ge(xT_hi_ready, 2 * c + k - 1)
                dve.tensor_tensor(lo[:, k, cols], X_BANK[k][:], hi[:, k, cols].bitcast(F32),
                                  ALU.subtract).then_inc(xT_ready, 1)

            def link(count):
                dve.wait_ge(route, count)

            def take_logits(c):
                t = slice(c * TC, (c + 1) * TC)
                dve.wait_ge(logits_made, c + 1)
                dve.tensor_scalar(logits[:, t, :], X_BANK[0][:, 0:TC * E].rearrange("p (t e) -> p t e", e=E),
                                  RSCALE, None, ALU.mult).then_inc(logits_ready, 1)
                dve.wait_ge(logits_ready, c + 1)
                dve.tensor_tensor(biased[:, t, :], logits[:, t, :],
                                  rb_sb[:].rearrange("p (o e) -> p o e", o=1).to_broadcast([128, TC, E]),
                                  ALU.add).then_inc(route, 1)

            def routing(c):
                link(3 * c + 1)
                for i in range(c * TC, (c + 1) * TC):
                    last = dve.max(top[:, i, :], biased[:, i, :])
                last.then_inc(route, 1)
                link(3 * c + 2)
                for i in range(c * TC, (c + 1) * TC):
                    last = dve.max_index(top_at[:, i, :], top[:, i, :], biased[:, i, :])
                last.then_inc(route, 1)

            def units(n, ms=range(MH)):
                for m in ms:
                    count = MH * n + m + 1
                    dve.wait_ge(tanh_ready, count)
                    wait(dve, hidden_ready, count - 1)
                    dve.scalar_tensor_tensor(gate[:], tanh[:, m % 2, :], 1.0, H_BANK[0][m % 2][:],
                                             ALU.add, ALU.mult).then_inc(gate_ready, 1)
                    dve.wait_ge(gate_ready, count)
                    dve.wait_ge(a1_made, count)
                    wait(dve, h_ready, count - 2)
                    dve.scalar_tensor_tensor(hidden[:, m % 2, :], gate[:], 0.5, H_BANK[1][m % 2][:],
                                             ALU.mult, ALU.mult).then_inc(hidden_ready, 1)

            def add_y(n, c, e, ts=range(TC)):
                for t in ts:
                    dve.wait_ge(y_made, TC * n + t + 1)
                    at = bass.ds(c * TC + t, 1)
                    dst = acc[:, at, :].rearrange("p o d -> p (o d)")
                    dve.scalar_tensor_tensor(dst, Y_BANK[t % 2][:, 0:D],
                                             share[:, bass.ds(e, 1), at].rearrange("p a b -> p (a b)"), dst,
                                             ALU.mult, ALU.add).then_inc(y_added, 1)

            def pick_two():
                n = 3 * CHUNKS
                link(n)
                dve.tensor_copy(top_atf[:], top_at[:, :, 0:2]).then_inc(route, 1)
                link(n + 1)
                all_e = iota[:].rearrange("p (o e) -> p o e", o=1).to_broadcast([128, TILES, E])
                for i in range(2):
                    last = dve.tensor_tensor(pick[:, i], all_e, top_atf[:, :, i:i + 1].to_broadcast([128, TILES, E]),
                                             ALU.is_equal)
                last.then_inc(route, 1)

            def their_logits():
                n = 3 * CHUNKS + 2
                link(n)
                for i in range(2):
                    last = dve.tensor_tensor(picked[:, i], pick[:, i], logits[:], ALU.mult)
                last.then_inc(route, 1)
                link(n + 1)
                for i in range(2):
                    last = dve.tensor_reduce(chosen[:, i, :], picked[:, i], AX.X, ALU.add)
                last.then_inc(route, 1)
                link(n + 2)
                dve.tensor_tensor(most[:], chosen[:, 0, :], chosen[:, 1, :], ALU.max).then_inc(route, 1)
                link(n + 3)
                for i in range(2):
                    last = dve.tensor_tensor(chosen[:, i, :], chosen[:, i, :], most[:], ALU.subtract)
                last.then_inc(chosen_ready, 1)

            def softmax_sum():
                n = 3 * CHUNKS + 5
                dve.wait_ge(chosen_exp, 1)
                dve.tensor_tensor(total[:], chosen[:, 0, :], chosen[:, 1, :], ALU.add).then_inc(route, 1)
                link(n + 1)
                dve.reciprocal(total_inv[:], total[:]).then_inc(route, 1)
                link(n + 2)
                for i in range(2):
                    last = dve.tensor_tensor(chosen[:, i, :], chosen[:, i, :], total_inv[:], ALU.mult)
                last.then_inc(route, 1)

            def shares():
                n = 3 * CHUNKS + 8
                link(n)
                for i in range(2):
                    last = dve.tensor_tensor(picked[:, i], pick[:, i],
                                             chosen[:, i, :].rearrange("p (t o) -> p t o", o=1).to_broadcast([128, TILES, E]),
                                             ALU.mult)
                last.then_inc(route, 1)
                link(n + 1)
                dve.tensor_tensor(share[:, 1:, :].rearrange("p e t -> p t e"), picked[:, 0], picked[:, 1],
                                  ALU.add).then_inc(route, 1)
                link(n + 2)

            statistics(1)
            for c in range(CHUNKS):
                more = c + 1 < CHUNKS
                take_logits(c)
                if c == 0:
                    dve.wait_ge(consts, 2)
                    dve.wait_ge(x1_loaded[0], 16)
                units(c, [0])
                if more:
                    normed(c + 1)
                    units(c, [1, 2])
                    for k in range(2):
                        lo_of_x(c + 1, k)
                else:
                    routing(c)
                    units(c, [1])
                    pick_two()
                    units(c, [2])
                    their_logits()
                units(c, [3])
                for t in range(TC):
                    if c > 0:
                        add_y(c - 1, c - 1, 0, [t])
                    if not more and t == 0:
                        softmax_sum()
                    if not more and t == 1:
                        shares()
                if more:
                    routing(c)
                if c + 2 < CHUNKS:
                    statistics(c + 2)

            def step(n, c, buf, e, k, prev, last):
                units(n)
                if k == 0:
                    add_y(n - 1, CHUNKS - 1, e)
                else:
                    add_y(n - 1, c - 1, e + 1)

            routed(dve, step)
            add_y(CHUNKS * (E + 1) - 1, CHUNKS - 1, E)

        @block.tensor
        def _(pe):
            def product(o, pairs):
                for n, (lhsT, rhs) in enumerate(pairs):
                    mm = pe.matmul(o, lhsT, rhs, start=(n == 0), stop=(n == len(pairs) - 1))
                return mm

            def transposed(c):
                pe.wait_ge(xn_ready, c)
                wait(pe, xT_ready, 2 * (c - 1))
                wait(pe, logits_ready, c)
                for k in range(2):
                    for t in range(TC):
                        mm = pe.transpose(X_BANK[k][:, t * 128:(t + 1) * 128], xn[:, t, k * 128:(k + 1) * 128], ident[:])
                    mm.then_inc(xT_made, 1)

            def router(c):
                hi, lo, cols = tokens(c)
                for t in range(TC):
                    tok = slice(t * 128, (t + 1) * 128)
                    mm = product(X_BANK[0][:, t * E:(t + 1) * E],
                                 [(v[:, k, cols][:, tok], w[:, k, :]) for k in range(2)
                                  for v, w in ((hi, wr_hi), (lo, wr_hi), (hi, wr_lo))])
                mm.then_inc(logits_made, 1)

            def up(n, c, buf):
                hi, lo, tok = tokens(c)
                for m in range(MH):
                    wait(pe, hidden_ready, MH * n + m - 1)
                    for o, base, made in ((H_BANK[0], 1024, a3_made), (H_BANK[1], 0, a1_made)):
                        cols = [slice(base + k * 512 + m * 128, base + k * 512 + m * 128 + 128) for k in range(2)]
                        product(o[m % 2][:], [(w[:, cols[k]], v[:, k, tok]) for k in range(2)
                                              for w, v in ((w_hi[buf], hi), (w_hi[buf], lo), (w_lo[buf], hi))]
                                ).then_inc(made, 1)
                    if isinstance(n, int) and n < CHUNKS - 1 and m == 2:
                        transposed(n + 1)

            def down(n, buf, s):
                pe.wait_ge(h_ready, MH * (n + 1))
                for t in range(TC):
                    wait(pe, y_added, TC * n + t - 1)
                    tok = slice(t * 128, (t + 1) * 128)
                    w2 = [slice(2048 + k * D, 2048 + (k + 1) * D) for k in range(MH)]
                    product(Y_BANK[t % 2][:, 0:D],
                            [(h[s][:, k, tok], w[buf][:, w2[k]]) for k in range(MH)
                             for h, w in ((hT_hi, w_hi), (hT_lo, w_hi), (hT_hi, w_lo))]).then_inc(y_made, 1)

            for c in range(CHUNKS):
                wait(pe, xT_ready, 2 * c)
                router(c)
                up(c, c, 1)
                if c > 0:
                    down(c - 1, 1, (c - 1) % 2)

            def step(n, c, buf, e, k, prev, last):
                if k == 0:
                    pe.wait_ge(piece_lo, PIECES * (e + 1))
                s = (CHUNKS + CHUNKS * buf + k) % 2
                up(n, c, buf)
                down(n - 1, 1 - buf if k == 0 else buf, 1 - s)

            routed(pe, step)
            down(CHUNKS * (E + 1) - 1, 1, (2 * CHUNKS + CHUNKS - 1) % 2)


_INS = ['x', 'ctx_768', 'L0_xattn_Wq', 'L0_xattn_Wk', 'L0_xattn_Wv', 'L0_xattn_Wout', 'L0_xattn_bout',
        'L0_ffn_Wr', 'L0_ffn_rb', 'L0_ffn_W1', 'L0_ffn_W2', 'L0_ffn_W3', 'L0_ffn_Ws1', 'L0_ffn_Ws2', 'L0_ffn_Ws3']


def kernel(**inputs):
    import numpy as _np
    import concourse.bacc as _bacc
    from concourse import mybir as _mybir
    from concourse.bass_utils import run_bass_kernel_spmd as _run

    nc = _bacc.Bacc("TRN2", target_bir_lowering=False, num_devices=1)
    arrays, args = {}, []
    for name in _INS:
        a = _np.ascontiguousarray(inputs[name])
        arrays[f"in_{name}"] = a
        args.append(nc.dram_tensor(f"in_{name}", a.shape, _mybir.dt.from_np(a.dtype), kind="ExternalInput").ap())
    out = nc.dram_tensor("out_0", inputs["x"].shape, _mybir.dt.float32, kind="ExternalOutput").ap()
    build(nc, *args, out)
    r = _run(nc, [arrays], core_ids=[0])
    return r.results[0]["out_0"]
```

```python
from contextlib import ExitStack

import concourse.bass as bass
from concourse import mybir

F32 = mybir.dt.float32
F32R = mybir.dt.float32r
U32 = mybir.dt.uint32
ALU = mybir.AluOpType
ACT = mybir.ActivationFunctionType
AX = mybir.AxisListType

EPS = 1e-5


def wait(eng, sem, count):
    if not isinstance(count, int) or count > 0:
        eng.wait_ge(sem, count)


UNIT_BANKS = 3
PROLOGUE = ["c0", "c1", "k0", "k1", "k2", "k3", "v0", "xt0", "xt1", "v1", "q0", "v2"]
EVEN = [([], ["c0", "c1"]), ([], ["q1", "k0"]), ([], ["k2"]), ([], ["k1", "v0"]),
        ([], ["wout"]), ([], ["v2", "xt0"]), ([], ["xt1"]), ([], ["v1", "k3"])]
ODD = [([], ["c0", "c1"]), ([], []), ([], ["k0"]), (["v1"], []),
       ([], ["v0", "k3"]), ([], ["q0"]), ([], ["v2", "k2"]), (["wout"], ["k1"])]


def slots_of(p, odd, last):
    full = ODD if odd else EVEN
    drop = set()
    if not odd and isinstance(p, int) and p == 0:
        drop.add("wout")
    if last and odd:
        return [([], []), ([], ["t0"]), ([], ["t1"]), ([], []), ([], ["wout"]), ([], []), ([], []), ([], [])]
    if last:
        drop |= {"xt0", "xt1"}
    return [tuple([u for u in part if u not in drop] for part in slot) for slot in full]


def names_of(p, odd, last):
    return [u for early, late in slots_of(p, odd, last) for u in early + late]


def count_of(p, odd, last, name, kinds):
    def among(names):
        return sum(u[0] in kinds for u in names)

    if isinstance(p, int) and p == 0:
        before = among(PROLOGUE)
    else:
        before = among(PROLOGUE) - ("w" in kinds) + among(names_of(1, False, False) + names_of(1, True, False)) * p
    if odd:
        before = before + among(names_of(p, False, last))
    names = names_of(p, odd, last)
    return before + among(names[: names.index(name) + 1])


ALL = "xckqvtw"
HI = "xckqvt"
DONE = "xckqtw"


def unit_count(p, odd, last, name):
    return count_of(p, odd, last, name, ALL)


def split_count(p, odd, last, name):
    return count_of(p, odd, last, name, HI)


def done_count(p, odd, last, name):
    return count_of(p, odd, last, name, DONE)


def prologue_count(n, kinds):
    return sum(u[0] in kinds for u in PROLOGUE[:n])


def bank_of(p, odd, last, name):
    q = p if isinstance(p, int) else 1
    return (unit_count(q, odd, last, name) - 1) % UNIT_BANKS


def bank_before(p, odd, last, name):
    before = names_of(p, odd, last)
    at = before.index(name) - UNIT_BANKS
    if at >= 0:
        where = (p, odd, last)
    elif odd:
        before, where = names_of(p, False, last), (p, False, last)
    elif isinstance(p, int) and p == 0:
        n = len(PROLOGUE) + at
        kinds = HI if PROLOGUE[n][0] == "v" else DONE
        return kinds == DONE, prologue_count(n + 1, kinds)
    else:
        before, where = names_of(p - 1, True, False), (p - 1, True, False)
    u = before[at]
    return (False, split_count(*where, u)) if u[0] == "v" else (True, done_count(*where, u))


def kv_count(p, odd, last, name):
    if odd or name == "q1":
        return done_count(p, False, last, name)
    if isinstance(p, int) and p == 0:
        return prologue_count(PROLOGUE.index(name) + 1, DONE)
    return done_count(p - 1, True, False, name)


def build(nc, x, ctx, Wq, Wk, Wv, Wout, bout, Wr, rb, W1, W2, W3, Ws1, Ws2, Ws3, out):
    B, N, D = x.shape
    _, M, C = ctx.shape
    INNER = Wq.shape[1]
    HEADS, DH = 8, INNER // 8
    E, _, H = W1.shape
    TOKENS = B * N
    KR = 125
    KT = M // KR
    ME = M + 1
    CT = C - 128
    PAIRS = B // 2
    N2 = 2 * N
    assert KT * KR == M and CT == 64 and DH == 64 and D == 256 and B % 2 == 0
    QSCALE = DH ** -0.5
    RSCALE = D ** -0.5
    TILES = TOKENS // 128
    CHUNK = 512
    CHUNKS = TOKENS // CHUNK
    TC = CHUNK // 128
    MH = H // 128
    PIECES = 6
    assert CHUNKS == 7 and TILES == 28 and MH == 4

    xf = x.rearrange("b n d -> (b n) d")
    outf = out.rearrange("b n d -> (b n) d")
    x1_dram = nc.dram_tensor("x1_scratch", (TOKENS, D), F32, kind="Internal").ap()

    top = ExitStack()
    sb = lambda name, shape, dt=F32, at=top: at.enter_context(nc.sbuf_tensor(name, shape, dt))
    sem = lambda name: top.enter_context(nc.semaphore(name))

    with top:
        stage = sb("stage", [128, 4096])
        w_hi1 = sb("w_hi1", [128, PIECES * 512], F32R)
        w_lo1 = sb("w_lo1", [128, PIECES * 512], F32R)
        ident = sb("ident", [128, 128])
        x1 = [sb(f"x1_{i}", [N, D]) for i in range(2)]
        x1_first = sb("x1_first", [128, TC, D])
        xn2 = sb("xn2", [128, TC, D])
        stats2, mean_var2 = sb("stats2", [128, TC, 6]), sb("mean_var2", [128, TC, 2])
        var_eps2, rstd2 = sb("var_eps2", [128, TC]), sb("rstd2", [128, TC])
        minus_half2, eps2 = sb("minus_half2", [128, TC]), sb("eps2", [128, TC])
        firstT_hi, firstT_lo = sb("firstT_hi", [128, 2, CHUNK], F32R), sb("firstT_lo", [128, 2, CHUNK], F32R)
        wr, rb_sb = sb("wr", [128, 2, E]), sb("rb_sb", [128, E])
        wr_split = sb("wr_split", [128, 2, 2 * E], F32R)
        first_logits = sb("first_logits", [128, TC * 2 * E])
        bank = [top.enter_context(nc.psum_tensor(f"bank{i}", [128, 512], F32)) for i in range(8)]

        weights_in = [None, sem("weights_in1"), sem("weights_in2")]
        bout_in = sem("bout_in")
        x1_stored = [sem("x1_stored0"), sem("x1_stored1")]
        router_in = sem("router_in")
        sw_hi, sw_lo = sem("sw_hi"), sem("sw_lo")

        def load_expert(eng, w1, w3, w2, s):
            eng.dma_start(stage[:, 0:1024].rearrange("p (k n) -> p k n", k=2),
                          w1.rearrange("(k p) n -> p k n", p=128)).then_inc(s, 16)
            eng.dma_start(stage[:, 1024:2048].rearrange("p (k n) -> p k n", k=2),
                          w3.rearrange("(k p) n -> p k n", p=128)).then_inc(s, 16)
            eng.dma_start(stage[:, 2048:3072].rearrange("p (k n) -> p k n", k=4),
                          w2.rearrange("(k p) n -> p k n", p=128)).then_inc(s, 16)

        attention(nc, locals())
        experts(nc, locals())


def attention(nc, g):
    (x, ctx, Wq, Wk, Wv, Wout, bout, Ws1, Ws2, Ws3) = (g[k] for k in "x ctx Wq Wk Wv Wout bout Ws1 Ws2 Ws3".split())
    (N, D, M, ME, INNER, HEADS, DH, KR, KT, CT, PAIRS, N2, QSCALE) = (
        g[k] for k in "N D M ME INNER HEADS DH KR KT CT PAIRS N2 QSCALE".split())
    (stage, w_hi1, w_lo1, ident, bank, weights_in, bout_in, x1, x1_stored, sw_hi, sw_lo, x1_dram, load_expert) = (
        g[k] for k in "stage w_hi1 w_lo1 ident bank weights_in bout_in x1 x1_stored sw_hi sw_lo x1_dram load_expert".split())
    (x1_first, xn2, stats2, mean_var2, var_eps2, rstd2, minus_half2, eps2, firstT_hi, firstT_lo) = (
        g[k] for k in "x1_first xn2 stats2 mean_var2 var_eps2 rstd2 minus_half2 eps2 firstT_hi firstT_lo".split())
    (wr, rb_sb, wr_split, first_logits, router_in, W1, W2, W3, Wr, rb, PIECES, TC, CHUNK, E) = (
        g[k] for k in "wr rb_sb wr_split first_logits router_in W1 W2 W3 Wr rb PIECES TC CHUNK E".split())

    own = ExitStack()
    sb = lambda name, shape, dt=F32: own.enter_context(nc.sbuf_tensor(name, shape, dt))
    sem = lambda name: own.enter_context(nc.semaphore(name))
    with own:
        wq_hi, wq_lo = sb("wq_hi", [128, 2, INNER], F32R), sb("wq_lo", [128, 2, INNER], F32R)
        wk_hi, wk_lo = sb("wk_hi", [128, 2, INNER], F32R), sb("wk_lo", [128, 2, INNER], F32R)
        wv_hi, wv_lo = sb("wv_hi", [128, 2, INNER], F32R), sb("wv_lo", [128, 2, INNER], F32R)
        wo_hi, wo_lo = sb("wo_hi", [128, 4, D], F32R), sb("wo_lo", [128, 4, D], F32R)
        bout_sb = sb("bout_sb", [N, D])

        x_in = sb("x_in", [N, 2, D])
        xn = sb("xn", [N, 2, D])
        stats = sb("stats", [N, 2, 6])
        mean_var = sb("mean_var", [N, 2, 2])
        var_eps = sb("var_eps", [N, 2])
        minus_half, eps, one = sb("minus_half", [N, 2]), sb("eps", [N, 2]), sb("one", [128, 1])
        rstd = sb("rstd", [N, 2])
        xT_hi, xT_lo = sb("xT_hi", [128, 2, N2], F32R), sb("xT_lo", [128, 2, N2], F32R)
        ctx_in = [sb(f"ctx_in{i}", [KR, KT, 256]) for i in range(2)]
        cT_hi, cT_lo = sb("cT_hi", [128, ME], F32R), sb("cT_lo", [128, ME], F32R)
        cT_tail = sb("cT_tail", [128, ME], F32R)
        q_hi, q_lo = sb("q_hi", [128, HEADS, 2, N], F32R), sb("q_lo", [128, HEADS, 2, N], F32R)
        keys = [sb(f"keys{i}", [128, HEADS, ME], F32R) for i in range(2)]
        v_hi = [sb(f"v_hi{i}", [KR, KT, INNER], F32R) for i in range(2)]
        v_lo = [sb(f"v_lo{i}", [KR, KT, INNER], F32R) for i in range(2)]
        v_raw = [sb(f"v_raw{i}", [KR, INNER]) for i in range(2)]
        probs = sb("probs", [N, 4, M])
        neg_max, row_sum, inv_sum = sb("neg_max", [N, 16]), sb("row_sum", [N, 16]), sb("inv_sum", [N, 16])
        pT_hi = sb("pT_hi", [KR, 2, KT, 2, N], F32R)
        pT_lo = sb("pT_lo", [KR, 2, KT, 2, N], F32R)
        oT_hi = [sb(f"oT_hi{i}", [128, 4, N], F32R) for i in range(2)]
        oT_lo = [sb(f"oT_lo{i}", [128, 4, N], F32R) for i in range(2)]
        x_res = [sb(f"x_res{i}", [N, D]) for i in range(2)]
        S_BANK, PT_BANK, O_BANK, U_BANK = bank[0:2], bank[2:4], bank[4], bank[5:8]

        x_loaded = sem("x_loaded")
        ctx_loaded = [sem("ctx_loaded0"), sem("ctx_loaded1")]
        res_loaded = [sem("res_loaded0"), sem("res_loaded1")]
        norm_consts, ident_zero = sem("norm_consts"), sem("ident_zero")
        zeros_ready, q_zeros = sem("zeros_ready"), sem("q_zeros")
        ident_ready = sem("ident_ready")
        aw_in = {kind: sem(f"aw_in_{kind}") for kind in "kvqo"}
        aw_hi = sem("aw_hi")
        aw_lo = {kind: sem(f"aw_lo_{kind}") for kind in "kvqo"}
        stats_done, var_ready, var_eps_ready, rstd_ready, xn_ready = (
            sem(n) for n in "stats_done var_ready var_eps_ready rstd_ready xn_ready".split())
        unit_made, unit_hi, unit_done = sem("unit_made"), sem("unit_hi"), sem("unit_done")
        v_hi_ready, v_ready = sem("v_hi_ready"), sem("v_ready")
        res_biased = sem("res_biased")
        scores_made, max_ready, exp_ready, inv_ready, probs_ready = (
            sem(n) for n in "scores_made max_ready exp_ready inv_ready probs_ready".split())
        first_loaded, first_stats, first_var, first_var_eps, first_rstd, first_normed = (
            sem("first_" + n) for n in "loaded stats var var_eps rstd normed".split())
        norm_consts2, wr_hi_ready, wr_ready = sem("norm_consts2"), sem("wr_hi_ready"), sem("wr_ready")
        pT_made, pT_hi_ready, pT_ready = sem("pT_made"), sem("pT_hi_ready"), sem("pT_ready")
        o_made, o_hi_ready, o_ready = sem("o_made"), sem("o_hi_ready"), sem("o_ready")

        AW = [("k", 0), ("k", 1), ("v", 0), ("v", 1), ("q", 0), ("q", 1), ("o", 0), ("o", 1)]
        AW_LOADS = {"k": 48, "v": 48, "q": 32, "o": 16}
        W_HI = {"q": wq_hi, "k": wk_hi, "v": wv_hi, "o": wo_hi}
        W_LO = {"q": wq_lo, "k": wk_lo, "v": wv_lo, "o": wo_lo}

        def piece(t, kind, i):
            return t[:, 2 * i:2 * i + 2, :] if kind == "o" else t[:, i, :]

        def staged(n, kind):
            s = stage[:, n * 512:(n + 1) * 512]
            return s.rearrange("p (k n) -> p k n", k=2) if kind == "o" else s

        def split_lo(eng, n):
            kind, i = AW[n]
            eng.wait_ge(aw_hi, n + 1)
            rows = slice(0, 64) if kind in "kv" and i == 1 else slice(0, 128)
            lo, hi, w = piece(W_LO[kind], kind, i)[rows], piece(W_HI[kind], kind, i)[rows].bitcast(F32), staged(n, kind)[rows]
            if kind == "q":
                eng.scalar_tensor_tensor(lo, w, QSCALE, hi, ALU.mult, ALU.subtract).then_inc(aw_lo[kind], 1)
            else:
                eng.tensor_tensor(lo, w, hi, ALU.subtract).then_inc(aw_lo[kind], 1)

        def v_count(p, odd, last, name):
            if name[0] != "v":
                return None, None
            return (count_of(p, odd, last, name, "v"),
                    (count_of(p if isinstance(p, int) else 1, odd, last, name, "v") - 1) % 2)

        def heads_of(name, half):
            first = 4 * int(name[1]) + half
            return slice(first, first + 3, 2)

        def ps_q(ps, rows):
            return ps[rows, 0:2 * N2].rearrange("p (m b n) -> p m b n", m=2, b=2)

        def rounds(eng, body):
            body(0, False)
            with eng.Fori(1, PAIRS - 1) as p:
                body(p, False)
            body(PAIRS - 1, True)

        def ctx_rows(b):
            return ctx[bass.ds(b, 1), :, :].rearrange("o (t r) c -> r (o t) c", r=KR)

        def batch_of(b):
            return x[bass.ds(b, 1), :, :].rearrange("o r d -> (o r) d")

        def x_rows(b, n):
            return x[bass.ds(b, n), :, :].rearrange("b r d -> r b d")

        block = own.enter_context(nc.Block())

        @block.sync
        def _(sp):
            def load_ctx(b, i):
                rows = ctx_rows(b)
                sp.dma_start(ctx_in[i][:, :, 0:192], rows).then_inc(ctx_loaded[i], 16)
                sp.dma_start(ctx_in[i][:, :, 192:256], rows[:, :, 128:192]).then_inc(ctx_loaded[i], 16)

            def load_weight(w, n, kind, split_rows):
                sp.dma_start(stage[:, n * 512:(n + 1) * 512], w[0:128, :]).then_inc(aw_in[kind], 16)
                if split_rows:
                    sp.dma_start(stage[0:64, (n + 1) * 512:(n + 2) * 512], w[128:192, :]).then_inc(aw_in[kind], 16)
                    sp.dma_start(stage[64:128, (n + 1) * 512:(n + 2) * 512], w[128:192, :]).then_inc(aw_in[kind], 16)
                else:
                    sp.dma_start(stage[:, (n + 1) * 512:(n + 2) * 512], w[128:256, :]).then_inc(aw_in[kind], 16)

            load_ctx(0, 0)
            sp.dma_start(x_in[:], x_rows(0, 2)).then_inc(x_loaded, 16)
            load_weight(Wk, 0, "k", True)
            load_weight(Wv, 2, "v", True)
            load_weight(Wq, 4, "q", False)
            sp.dma_start(stage[:, 3072:4096].rearrange("p (k n) -> p k n", k=4),
                         Wout.rearrange("(k p) n -> p k n", p=128)).then_inc(aw_in["o"], 16)
            sp.dma_start(bout_sb[:], bout.rearrange("(o d) -> o d", o=1).to_broadcast([N, D])).then_inc(bout_in, 16)
            load_ctx(1, 1)
            sp.dma_start(wr[:], Wr.rearrange("(k p) e -> p k e", p=128)).then_inc(router_in, 16)
            sp.dma_start(rb_sb[:], rb.rearrange("(o e) -> o e", o=1).to_broadcast([128, E])).then_inc(router_in, 16)
            sp.dma_start(x_res[0][:], x[0]).then_inc(res_loaded[0], 16)
            sp.dma_start(x_res[1][:], x[1]).then_inc(res_loaded[1], 16)
            sp.wait_ge(xn_ready, 1)
            sp.dma_start(x_in[:], x_rows(2, 2)).then_inc(x_loaded, 16)
            sp.wait_ge(unit_made, PROLOGUE.index("c1") + 1)
            load_ctx(2, 0)
            sp.wait_ge(aw_hi, len(AW))
            for kind in "kvqo":
                sp.wait_ge(aw_lo[kind], 2)
            load_expert(sp, Ws1, Ws3, Ws2, weights_in[1])

            def store(b, i, count):
                sp.wait_ge(unit_done, count)
                sp.dma_start(x1_dram[bass.ds(b * N, N), :], x1[i][:]).then_inc(x1_stored[i], 16)

            def body(p, last):
                first = isinstance(p, int) and p == 0
                two_more = not isinstance(p, int) or p + 2 < PAIRS
                if not last:
                    sp.wait_ge(unit_made, unit_count(p, False, last, "c1"))
                    load_ctx(2 * p + 3, 1)
                if not first:
                    store(2 * p - 1, 1, done_count(p, False, last, "wout"))
                    sp.dma_start(x_res[1][:], batch_of(2 * p + 1)).then_inc(res_loaded[1], 16)
                if two_more:
                    sp.wait_ge(xn_ready, p + 2)
                    sp.dma_start(x_in[:], x_rows(2 * p + 4, 2)).then_inc(x_loaded, 16)
                    sp.wait_ge(unit_made, unit_count(p, True, last, "c1"))
                    load_ctx(2 * p + 4, 0)
                store(2 * p, 0, done_count(p, True, last, "wout"))
                if not last:
                    sp.dma_start(x_res[0][:], batch_of(2 * p + 2)).then_inc(res_loaded[0], 16)

            body(0, False)
            with sp.Fori(1, PAIRS - 2) as p:
                body(p, False)
            body(PAIRS - 2, False)
            for i in range(2):
                sp.wait_ge(x1_stored[i], 16 * (PAIRS - 2 + i))
            sp.dma_start(x1_first[:], x1_dram[0:CHUNK, :].rearrange("(t p) d -> p t d", p=128)).then_inc(first_loaded, 16)
            body(PAIRS - 1, True)
            sp.wait_ge(unit_done, done_count(PAIRS - 1, True, True, names_of(PAIRS - 1, True, True)[-1]) + 2)
            sp.dma_start(x1_dram[(2 * PAIRS - 1) * N:2 * PAIRS * N, :], x1[1][:]).then_inc(x1_stored[1], 16)
            sp.wait_ge(sw_hi, PIECES)
            sp.wait_ge(sw_lo, PIECES)
            load_expert(sp, W1[0], W3[0], W2[0], weights_in[2])

        @block.gpsimd
        def _(pool):
            pool.memset(ident[:], 0.0).then_inc(ident_zero, 1)
            pool.memset(minus_half[:], -0.5).then_inc(norm_consts, 1)
            pool.memset(eps[:], EPS).then_inc(norm_consts, 1)
            pool.memset(one[:], 1.0).then_inc(norm_consts, 1)
            pool.memset(minus_half2[:], -0.5).then_inc(norm_consts2, 1)
            pool.memset(eps2[:], EPS).then_inc(norm_consts2, 1)
            pool.wait_ge(ident_zero, 1)
            pool.affine_select(out=ident[:], in_=ident[:], compare_op=ALU.not_equal, fill=1.0, base=0,
                               pattern=[[-1, 128]], channel_multiplier=1).then_inc(ident_ready, 1)

            def rstd_of(n):
                pool.wait_ge(var_ready, n)
                pool.tensor_tensor(var_eps[:], mean_var[:, :, 1], eps[:], ALU.add).then_inc(var_eps_ready, 1)
                pool.wait_ge(var_eps_ready, n)
                pool.tensor_tensor(rstd[:], var_eps[:], minus_half[:], ALU.pow).then_inc(rstd_ready, 1)

            def split_values(name, b, n_hi, n_v, at_v):
                t = int(name[1])
                pool.wait_ge(unit_hi, n_hi)
                pool.tensor_tensor(v_hi[b][:, t, :], v_raw[at_v][:], one[0:KR, :].to_broadcast([KR, INNER]),
                                   ALU.mult).then_inc(v_hi_ready, 1)
                pool.wait_ge(v_hi_ready, n_v)
                pool.tensor_tensor(v_lo[b][:, t, :], v_raw[at_v][:], v_hi[b][:, t, :].bitcast(F32),
                                   ALU.subtract).then_inc(v_ready, 1)

            def add_bout(i, n):
                pool.wait_ge(res_loaded[i], 16 * n)
                pool.tensor_tensor(x_res[i][:], x_res[i][:], bout_sb[:], ALU.add).then_inc(res_biased, 1)

            pool.wait_ge(norm_consts, 3)
            rstd_of(1)
            for n in (2, 3):
                split_lo(pool, n)
            for n, name in enumerate(PROLOGUE):
                if name[0] == "v":
                    n_v = prologue_count(n + 1, "v")
                    split_values(name, 0, prologue_count(n + 1, HI), n_v, (n_v - 1) % 2)
            for n in (6, 7):
                split_lo(pool, n)
            pool.wait_ge(bout_in, 16)
            add_bout(0, 1)
            add_bout(1, 1)

            def body(p, last):
                for s in range(16):
                    pool.wait_ge(inv_ready, 16 * p + s + 1)
                    pool.tensor_tensor(probs[:, s % 4, :], probs[:, s % 4, :],
                                       inv_sum[:, s:s + 1].to_broadcast([N, M]), ALU.mult).then_inc(probs_ready, 1)
                    odd = bool(s // 8)
                    early, late = slots_of(p, odd, last)[s % 8]
                    for name in early + late:
                        if name[0] == "v":
                            split_values(name, 0 if odd else 1, split_count(p, odd, last, name),
                                         *v_count(p, odd, last, name))
                    if s == 2 and not last:
                        rstd_of(p + 2)
                    if s == 5 and last:
                        pool.wait_ge(norm_consts2, 2)
                        pool.wait_ge(first_var, 1)
                        pool.tensor_tensor(var_eps2[:], mean_var2[:, :, 1], eps2[:], ALU.add).then_inc(first_var_eps, 1)
                        pool.wait_ge(first_var_eps, 1)
                        pool.tensor_tensor(rstd2[:], var_eps2[:], minus_half2[:], ALU.pow).then_inc(first_rstd, 1)
                    if s in (1, 9) and not (isinstance(p, int) and p == 0):
                        add_bout(s // 8, p + 1)
                if isinstance(p, int) and p == 0:
                    pool.wait_ge(weights_in[1], 48)
                    for j in range(PIECES):
                        cols = slice(j * 512, (j + 1) * 512)
                        pool.wait_ge(sw_hi, j + 1)
                        pool.tensor_tensor(w_lo1[:, cols], stage[:, cols], w_hi1[:, cols].bitcast(F32),
                                           ALU.subtract).then_inc(sw_lo, 1)

            rounds(pool, body)

        @block.scalar
        def _(act):
            def split_hi(n):
                kind, i = AW[n]
                act.wait_ge(aw_in[kind], AW_LOADS[kind])
                act.activation(piece(W_HI[kind], kind, i), staged(n, kind), ACT.Copy,
                               scale=QSCALE if kind == "q" else 1.0).then_inc(aw_hi, 1)

            def unit(n_made, name, b, ps, n_v=None, at_v=None):
                act.wait_ge(unit_made, n_made)
                if name[0] == "x":
                    j = int(name[2])
                    act.activation(xT_hi[:, :, j * N:(j + 1) * N],
                                   ps[:, 0:2 * N].rearrange("p (k n) -> p k n", k=2), ACT.Copy).then_inc(unit_hi, 1)
                elif name[0] == "t":
                    act.activation(firstT_hi[:, int(name[1]), :], ps[:], ACT.Copy).then_inc(unit_hi, 1)
                elif name == "c0":
                    act.activation(cT_hi[:, 0:M], ps[:, 0:M], ACT.Copy).then_inc(unit_hi, 1)
                elif name == "c1":
                    act.activation(cT_tail[:, 0:M], ps[:, 0:M], ACT.Copy).then_inc(unit_hi, 1)
                elif name[0] == "q":
                    for half in range(2):
                        rows, heads = slice(64 * half, 64 * half + 64), heads_of(name, half)
                        for to in (slice(0, 64), slice(64, 128)):
                            last = act.activation(q_hi[to, heads, :, :], ps_q(ps, rows), ACT.Copy)
                    last.then_inc(unit_hi, 1)
                elif name[0] == "k":
                    for half in range(2):
                        rows = slice(64 * half, 64 * half + 64)
                        last = act.activation(keys[b][rows, 2 * int(name[1]) + half, :], ps[rows, 0:ME], ACT.Copy)
                    last.then_inc(unit_hi, 1)
                elif name[0] == "v":
                    wait(act, v_ready, n_v - 2)
                    act.activation(v_raw[at_v][:], ps[0:KR, :], ACT.Copy).then_inc(unit_hi, 1)

            for n, name in enumerate(PROLOGUE):
                for i in {"k0": range(6), "k1": (6, 7)}.get(name, ()):
                    split_hi(i)
                n_v = prologue_count(n + 1, "v")
                unit(n + 1, name, 0, U_BANK[n % UNIT_BANKS], n_v, (n_v - 1) % 2)

            def o_part(a, j):
                act.wait_ge(o_made, a + 1)
                bk = O_BANK
                act.activation(oT_hi[j // 4][0:64, j % 4, :], bk[0:64, 0:N], ACT.Copy)
                act.activation(oT_hi[j // 4][64:128, j % 4, :], bk[64:128, N:N2], ACT.Copy).then_inc(o_hi_ready, 1)

            def slot(p, last, s, lead):
                gh = 16 * p + s
                odd = s // 8
                first = isinstance(p, int) and p == 0
                if lead:
                    act.wait_ge(max_ready, gh + 1)
                    wait(act, pT_made, gh - 3)
                    act.activation(probs[:, s % 4, :], S_BANK[s % 2][0:N, 0:M], ACT.Exp, bias=neg_max[:, s:s + 1],
                                   accum_out=row_sum[:, s:s + 1]).then_inc(exp_ready, 1)
                early, late = slots_of(p, bool(odd), last)[s % 8] if lead else ([], [])

                def run(names):
                    for name in names:
                        if name != "wout":
                            unit(unit_count(p, bool(odd), last, name), name, 1 - odd,
                                 U_BANK[bank_of(p, bool(odd), last, name)], *v_count(p, bool(odd), last, name))

                run(early)
                if not (first and s < 2) and s < 18:
                    t = s - 2
                    act.wait_ge(pT_made, gh - 1)
                    wait(act, o_made, 8 * p + t // 2 - 1)
                    act.activation(pT_hi[:, (t // 2) % 2, :, t % 2, :],
                                   PT_BANK[t % 2][0:KR, 0:KT * N].rearrange("p (t n) -> p t n", t=KT),
                                   ACT.Copy).then_inc(pT_hi_ready, 1)
                run(late)
                if s % 2 == 0 and not (first and s < 4):
                    o_part(8 * p + s // 2 - 2, (s // 2 - 2) % 8)

            def body(p, last):
                for s in range(16):
                    slot(p, last, s, True)
                if isinstance(p, int) and p == 0:
                    act.wait_ge(weights_in[1], 48)
                    for j in range(PIECES):
                        cols = slice(j * 512, (j + 1) * 512)
                        act.activation(w_hi1[:, cols], stage[:, cols], ACT.Copy).then_inc(sw_hi, 1)
                    act.wait_ge(router_in, 32)
                    act.activation(wr_split[:, :, 0:E], wr[:], ACT.Copy).then_inc(wr_hi_ready, 1)

            rounds(act, body)
            for s in range(16, 19):
                slot(PAIRS - 1, True, s, False)

        @block.vector
        def _(dve):
            def statistics(n):
                dve.wait_ge(x_loaded, 16 * n)
                dve.bn_stats(stats[:, 0, :], x_in[:, 0, :])
                dve.bn_stats(stats[:, 1, :], x_in[:, 1, :]).then_inc(stats_done, 1)
                dve.wait_ge(x_loaded, 16)
                dve.wait_ge(stats_done, n)
                dve.bn_aggr(mean_var[:, 0, :], stats[:, 0, :])
                dve.bn_aggr(mean_var[:, 1, :], stats[:, 1, :]).then_inc(var_ready, 1)

            def normed(n):
                dve.wait_ge(rstd_ready, n)
                dve.wait_ge(var_ready, n)
                for j in range(2):
                    last = dve.tensor_scalar(xn[:, j, :], x_in[:, j, :], mean_var[:, j, 0:1], rstd[:, j:j + 1],
                                             ALU.subtract, ALU.mult)
                last.then_inc(xn_ready, 1)

            def first_statistics():
                dve.wait_ge(first_loaded, 16)
                for t in range(TC):
                    last = dve.bn_stats(stats2[:, t, :], x1_first[:, t, :])
                last.then_inc(first_stats, 1)
                dve.wait_ge(first_stats, 1)
                for t in range(TC):
                    last = dve.bn_aggr(mean_var2[:, t, :], stats2[:, t, :])
                last.then_inc(first_var, 1)

            def unit(n_hi, name, b, ps):
                dve.wait_ge(unit_hi, n_hi)
                if name[0] == "x":
                    cols = slice(int(name[2]) * N, (int(name[2]) + 1) * N)
                    dve.tensor_tensor(xT_lo[:, :, cols], ps[:, 0:2 * N].rearrange("p (k n) -> p k n", k=2),
                                      xT_hi[:, :, cols].bitcast(F32), ALU.subtract).then_inc(unit_done, 1)
                elif name[0] == "t":
                    dve.tensor_tensor(firstT_lo[:, int(name[1]), :], ps[:], firstT_hi[:, int(name[1]), :].bitcast(F32),
                                      ALU.subtract).then_inc(unit_done, 1)
                elif name == "c0":
                    dve.tensor_tensor(cT_lo[:, 0:M], ps[:, 0:M], cT_hi[:, 0:M].bitcast(F32), ALU.subtract).then_inc(unit_done, 1)
                elif name == "c1":
                    dve.tensor_tensor(cT_tail[64:128, 0:M], ps[64:128, 0:M], cT_tail[64:128, 0:M].bitcast(F32),
                                      ALU.subtract).then_inc(unit_done, 1)
                elif name[0] == "q":
                    for half in range(2):
                        rows, heads = slice(64 * half, 64 * half + 64), heads_of(name, half)
                        last = dve.tensor_tensor(q_lo[rows, heads, :, :], ps_q(ps, rows),
                                                 q_hi[rows, heads, :, :].bitcast(F32), ALU.subtract)
                    last.then_inc(unit_done, 1)
                elif name[0] == "k":
                    for half in range(2):
                        rows, other, h = (slice(64 * half, 64 * half + 64), slice(64 - 64 * half, 128 - 64 * half),
                                          2 * int(name[1]) + half)
                        last = dve.tensor_tensor(keys[b][other, h, :], ps[rows, 0:ME], keys[b][rows, h, :].bitcast(F32),
                                                 ALU.subtract)
                    last.then_inc(unit_done, 1)

            def residual(count, i, n_res, n_store, ps):
                dve.wait_ge(unit_made, count)
                dve.wait_ge(res_biased, n_res)
                wait(dve, x1_stored[i], 16 * (n_store + i))
                dve.tensor_tensor(x1[i][:], ps[0:N, 0:D], x_res[i][:], ALU.add).then_inc(unit_done, 1)

            def zero_heads(t):
                for half in range(2):
                    dve.memset(t[64 * half:64 * half + 64, :, :, :].rearrange(
                        "p (m e) b n -> p m e (b n)", e=2)[:, :, 1 - half, :].bitcast(F32), 0.0).then_inc(q_zeros, 1)

            for t in (wk_lo, wv_lo):
                dve.memset(t[64:128, 1, :].bitcast(F32), 0.0).then_inc(zeros_ready, 1)
            for t in (cT_hi, cT_lo, cT_tail):
                dve.memset(t[:, M:ME].bitcast(F32), 0.0).then_inc(zeros_ready, 1)
            dve.memset(x1[1][:], 0.0).then_inc(x1_stored[1], 16)
            statistics(1)
            for n, name in enumerate(PROLOGUE):
                if name == "k0":
                    normed(1)
                    for i in (0, 1, 4, 5):
                        split_lo(dve, i)
                if name == "k1":
                    zero_heads(q_lo)
                if name[0] != "v":
                    unit(n + 1, name, 0, U_BANK[n % UNIT_BANKS])

            def run(p, odd, last, name):
                ps = U_BANK[bank_of(p, odd, last, name)]
                if name == "wout":
                    residual(unit_count(p, odd, last, name), 0 if odd else 1,
                             2 * p + 1 if odd else 2 * p, p if odd else p - 1, ps)
                elif name[0] != "v":
                    unit(split_count(p, odd, last, name), name, 0 if odd else 1, ps)

            def slot(p, last, s, lead):
                gh = 16 * p + s
                odd = bool(s // 8)
                first = isinstance(p, int) and p == 0
                if lead:
                    dve.wait_ge(scores_made, gh + 1)
                    dve.tensor_reduce(neg_max[:, s:s + 1], S_BANK[s % 2][0:N, 0:M], AX.X, ALU.max,
                                      negate=True).then_inc(max_ready, 1)
                if s == 0 and not first:
                    for name in ODD[7][1]:
                        run(p - 1, True, False, name)
                elif 0 < s <= 16 and not (last and s == 16):
                    was_odd = (s - 1) // 8 == 1
                    for name in slots_of(p, was_odd, last)[(s - 1) % 8][1]:
                        run(p, was_odd, last, name)
                if lead:
                    dve.wait_ge(exp_ready, gh + 1)
                    dve.reciprocal(inv_sum[:, s:s + 1], row_sum[:, s:s + 1]).then_inc(inv_ready, 1)
                if s % 2 == 1 and not (first and s < 5):
                    j = ((s - 1) // 2 - 2) % 8
                    dve.wait_ge(o_hi_ready, 8 * p + (s - 1) // 2 - 1)
                    dve.tensor_tensor(oT_lo[j // 4][0:64, j % 4, :], O_BANK[0:64, 0:N],
                                      oT_hi[j // 4][0:64, j % 4, :].bitcast(F32), ALU.subtract)
                    dve.tensor_tensor(oT_lo[j // 4][64:128, j % 4, :], O_BANK[64:128, N:N2],
                                      oT_hi[j // 4][64:128, j % 4, :].bitcast(F32), ALU.subtract).then_inc(o_ready, 1)
                for name in slots_of(p, odd, last)[s % 8][0] if lead else []:
                    run(p, odd, last, name)
                if not (first and s < 2) and s < 18:
                    t = s - 2
                    dve.wait_ge(pT_hi_ready, gh - 1)
                    dve.tensor_tensor(pT_lo[:, (t // 2) % 2, :, t % 2, :],
                                      PT_BANK[t % 2][0:KR, 0:KT * N].rearrange("p (t n) -> p t n", t=KT),
                                      pT_hi[:, (t // 2) % 2, :, t % 2, :].bitcast(F32),
                                      ALU.subtract).then_inc(pT_ready, 1)
                if s == 1 and lead and not last:
                    statistics(p + 2)
                if s == 4 and lead and not last:
                    normed(p + 2)
                if s == 3 and last:
                    first_statistics()
                if s == 7 and last:
                    dve.wait_ge(first_rstd, 1)
                    for t in range(TC):
                        mm = dve.tensor_scalar(xn2[:, t, :], x1_first[:, t, :], mean_var2[:, t, 0:1],
                                               rstd2[:, t:t + 1], ALU.subtract, ALU.mult)
                    mm.then_inc(first_normed, 1)
                if s == 12 and last:
                    dve.wait_ge(wr_hi_ready, 1)
                    dve.tensor_tensor(wr_split[:, :, E:], wr[:], wr_split[:, :, 0:E].bitcast(F32), ALU.subtract).then_inc(wr_ready, 1)

            def body(p, last):
                for s in range(16):
                    slot(p, last, s, True)

            rounds(dve, body)
            slot(PAIRS - 1, True, 16, False)
            n = unit_count(PAIRS - 1, True, True, names_of(PAIRS - 1, True, True)[-1]) + 1
            slot(PAIRS - 1, True, 17, False)
            dve.wait_ge(unit_made, n)
            dve.tensor_copy(first_logits[:], U_BANK[(n - 1) % UNIT_BANKS][:, 0:TC * 2 * E]).then_inc(unit_done, 1)
            for s in range(18, 20):
                slot(PAIRS - 1, True, s, False)
            residual(n + 1, 1, 2 * PAIRS, PAIRS - 1, U_BANK[n % UNIT_BANKS])

        @block.tensor
        def _(pe):
            def product(o, pairs):
                for n, (lhsT, rhs) in enumerate(pairs):
                    mm = pe.matmul(o, lhsT, rhs, start=(n == 0), stop=(n == len(pairs) - 1))
                return mm

            def unit(name, b, ps, before):
                if before:
                    pe.wait_ge(unit_done if before[0] else unit_hi, before[1])
                if name[0] == "x":
                    j = int(name[2])
                    for k in range(2):
                        mm = pe.transpose(ps[:, k * N:(k + 1) * N], xn[:, j, k * 128:(k + 1) * 128], ident[0:N, 0:N])
                elif name[0] == "t":
                    k = int(name[1])
                    for t in range(TC):
                        mm = pe.transpose(ps[:, t * 128:(t + 1) * 128], xn2[:, t, k * 128:(k + 1) * 128], ident[:])
                elif name[0] == "c":
                    c = int(name[1]) * 128
                    for t in range(KT):
                        mm = pe.transpose(ps[:, t * KR:(t + 1) * KR], ctx_in[b][:, t, c:c + 128], ident[0:KR, 0:KR])
                elif name[0] == "q":
                    for m in range(2):
                        cols = slice((2 * int(name[1]) + m) * 128, (2 * int(name[1]) + m + 1) * 128)
                        mm = product(ps[:, m * N2:(m + 1) * N2],
                                     [(w[:, k, cols], v[:, k, :]) for k in range(2)
                                      for w, v in ((wq_hi, xT_hi), (wq_hi, xT_lo), (wq_lo, xT_hi))])
                elif name[0] == "k":
                    cols = slice(int(name[1]) * 128, int(name[1]) * 128 + 128)
                    mm = product(ps[:, 0:ME], [(wk_hi[:, 0, cols], cT_hi[:]), (wk_hi[:, 0, cols], cT_lo[:]),
                                              (wk_lo[:, 0, cols], cT_hi[:]), (wk_hi[:, 1, cols], cT_tail[:]),
                                              (wk_lo[:, 1, cols], cT_tail[:])])
                elif name[0] == "v":
                    r = slice(int(name[1]) * KR, (int(name[1]) + 1) * KR)
                    mm = product(ps[0:KR, :], [(cT_hi[:, r], wv_hi[:, 0, :]), (cT_lo[:, r], wv_hi[:, 0, :]),
                                               (cT_hi[:, r], wv_lo[:, 0, :]), (cT_tail[:, r], wv_hi[:, 1, :]),
                                               (cT_tail[:, r], wv_lo[:, 1, :])])
                elif name == "router":
                    for t in range(TC):
                        tok = slice(t * 128, (t + 1) * 128)
                        mm = product(ps[:, t * 2 * E:(t + 1) * 2 * E],
                                     [(v[:, k, tok], wr_split[:, k, :]) for k in range(2)
                                      for v in (firstT_hi, firstT_lo)])
                elif name == "wout":
                    mm = product(ps[0:N, 0:D], [(o[b][:, k, :], w[:, k, :]) for k in range(4)
                                                for o, w in ((oT_hi, wo_hi), (oT_lo, wo_hi), (oT_hi, wo_lo))])
                mm.then_inc(unit_made, 1)

            pe.wait_ge(ident_ready, 1)
            for n, name in enumerate(PROLOGUE):
                if name == "xt0":
                    pe.wait_ge(xn_ready, 1)
                if name == "c0":
                    pe.wait_ge(ctx_loaded[0], 32)
                if name == "k0":
                    pe.wait_ge(zeros_ready, 5)
                    pe.wait_ge(aw_lo["k"], 2)
                    pe.wait_ge(unit_done, prologue_count(n, DONE))
                if name == "v0":
                    pe.wait_ge(aw_lo["v"], 2)
                if name == "q0":
                    pe.wait_ge(aw_lo["q"], 2)
                    pe.wait_ge(unit_done, prologue_count(PROLOGUE.index("xt1") + 1, DONE))
                before = None
                if n >= UNIT_BANKS:
                    kinds = HI if PROLOGUE[n - UNIT_BANKS][0] == "v" else DONE
                    before = (kinds == DONE, prologue_count(n - UNIT_BANKS + 1, kinds))
                unit(name, 0, U_BANK[n % UNIT_BANKS], before)
            pe.wait_ge(q_zeros, 2)

            def slot(p, last, s, lead):
                gh = 16 * p + s
                odd = bool(s // 8)
                first = isinstance(p, int) and p == 0
                h = s % 8
                if lead:
                    if s in (0, 4):
                        pe.wait_ge(unit_done, kv_count(p, False, last, f"q{s // 4}"))
                    pe.wait_ge(unit_done, kv_count(p, odd, last, f"k{h // 2}"))
                    wait(pe, exp_ready, gh - 1)
                    i, m = int(odd), h // 2
                    product(S_BANK[s % 2][0:N, 0:ME], [(q_hi[:, h, i, :], keys[i][:, h, :]),
                                                      (q_lo[:, h, i, :], keys[i][:, h, :])]).then_inc(scores_made, 1)
                early, late = slots_of(p, odd, last)[h] if lead else ([], [])

                def run(name):
                    if name == "xt0":
                        pe.wait_ge(xn_ready, p + 2)
                    if name == "c0":
                        pe.wait_ge(ctx_loaded[0 if odd else 1], 32 * (p + 2 if odd else p + 1))
                    if name == "k0":
                        pe.wait_ge(unit_done, done_count(p, odd, last, "c1"))
                    if name == "q0":
                        pe.wait_ge(unit_done, done_count(p, False, last, "xt1"))
                    if name == "t0":
                        pe.wait_ge(first_normed, 1)
                    if name == "wout" and first:
                        pe.wait_ge(aw_lo["o"], 2)
                    if name == "wout":
                        pe.wait_ge(o_ready, 8 * p + 4 if odd else 8 * p)
                    unit(name, 0 if odd else 1, U_BANK[bank_of(p, odd, last, name)], bank_before(p, odd, last, name))

                for name in early:
                    run(name)
                if not (first and s < 2) and s < 18:
                    t = s - 2
                    pe.wait_ge(probs_ready, gh - 1)
                    wait(pe, pT_ready, gh - 3)
                    for kt in range(KT):
                        mm = pe.transpose(PT_BANK[t % 2][0:KR, kt * N:(kt + 1) * N],
                                          probs[:, t % 4, kt * KR:(kt + 1) * KR], ident[0:N, 0:N])
                    mm.then_inc(pT_made, 1)
                for name in late:
                    run(name)
                if s % 2 == 0 and not (first and s < 4):
                    a = 8 * p + s // 2 - 2
                    j = (s // 2 - 2) % 8
                    i, m = j // 4, j % 4
                    pe.wait_ge(pT_ready, 2 * a + 2)
                    if m == 0:
                        pe.wait_ge(v_ready, KT * (2 * p + i + 1))
                    wait(pe, o_ready, a)
                    vh, vl, cols = v_hi[i], v_lo[i], slice(m * 128, (m + 1) * 128)
                    pt = [t[:, j % 2, :, :, :].rearrange("p t e n -> p t (e n)") for t in (pT_hi, pT_lo)]
                    product(O_BANK[:, 0:N2],
                            [(v[:, kt, cols], w[:, kt, :]) for kt in range(KT)
                             for v, w in ((vh, pt[0]), (vh, pt[1]), (vl, pt[0]))]).then_inc(o_made, 1)

            def body(p, last):
                for s in range(16):
                    slot(p, last, s, True)

            rounds(pe, body)
            slot(PAIRS - 1, True, 16, False)
            n = unit_count(PAIRS - 1, True, True, names_of(PAIRS - 1, True, True)[-1]) + 1
            pe.wait_ge(wr_ready, 1)
            pe.wait_ge(unit_done, done_count(PAIRS - 1, True, True, names_of(PAIRS - 1, True, True)[-1]))
            unit("router", 1, U_BANK[(n - 1) % UNIT_BANKS], None)
            for s in range(17, 19):
                slot(PAIRS - 1, True, s, False)
            pe.wait_ge(o_ready, 8 * PAIRS)
            unit("wout", 1, U_BANK[n % UNIT_BANKS], None)


def experts(nc, g):
    (W1, W2, W3, outf, x1_dram) = (g[k] for k in "W1 W2 W3 outf x1_dram".split())
    PAIRS, wr_split, first_logits, rb_sb, x1_first, x1_stored = (
        g[k] for k in "PAIRS wr_split first_logits rb_sb x1_first x1_stored".split())
    (xn, stats, mean_var, var_eps, rstd, minus_half, firstT_hi, firstT_lo) = (
        g[k] for k in "xn2 stats2 mean_var2 var_eps2 rstd2 minus_half2 firstT_hi firstT_lo".split())
    (D, E, H, TILES, CHUNK, CHUNKS, TC, MH, PIECES, RSCALE) = (
        g[k] for k in "D E H TILES CHUNK CHUNKS TC MH PIECES RSCALE".split())
    (stage, w_hi1, w_lo1, ident, bank, weights_in, load_expert) = (
        g[k] for k in "stage w_hi1 w_lo1 ident bank weights_in load_expert".split())

    own = ExitStack()
    sb = lambda name, shape, dt=F32: own.enter_context(nc.sbuf_tensor(name, shape, dt))
    sem = lambda name: own.enter_context(nc.semaphore(name))
    with own:
        w_hi = [sb("w_hi0", [128, PIECES * 512], F32R), w_hi1]
        w_lo = [sb("w_lo0", [128, PIECES * 512], F32R), w_lo1]
        acc = sb("acc", [128, TILES, D])
        REST = (CHUNKS - 1) * CHUNK
        xT_hi, xT_lo = sb("x2T_hi", [128, 2, REST], F32R), sb("x2T_lo", [128, 2, REST], F32R)
        hT_hi = [sb(f"hT_hi{i}", [128, MH, CHUNK], F32R) for i in range(2)]
        hT_lo = [sb(f"hT_lo{i}", [128, MH, CHUNK], F32R) for i in range(2)]
        tanh = x1_first[:].rearrange("p (m a) d -> p m (a d)", m=2)
        gate = sb("gate", [128, CHUNK])
        hidden = sb("hidden", [128, 2, CHUNK])
        part = sb("part", [128, TC, E])
        logits = sb("logits", [128, TILES, E])
        biased = sb("biased", [128, TILES, E])
        top = sb("top", [128, TILES, 8])
        top_at = sb("top_at", [128, TILES, 8], U32)
        top_atf = sb("top_atf", [128, TILES, 2])
        iota = sb("iota", [128, E])
        pick = sb("pick", [128, 2, TILES, E])
        picked = sb("picked", [128, 2, TILES, E])
        chosen = sb("chosen", [128, 2, TILES])
        most, total, total_inv = sb("most", [128, TILES]), sb("total", [128, TILES]), sb("total_inv", [128, TILES])
        share = sb("share", [128, 1 + E, TILES])
        H_BANK, Y_BANK, X_BANK = (bank[0:2], bank[2:4]), bank[4:6], bank[6:8]

        x1_loaded = [sem(f"x1_loaded{c}") for c in range(CHUNKS)]
        consts = sem("consts2")
        stats_done, var_ready, var_eps_ready, rstd_ready, xn_ready = (
            sem(n + "2") for n in "stats_done var_ready var_eps_ready rstd_ready xn_ready".split())
        xT_made, xT_hi_ready, xT_ready = sem("xT_made"), sem("xT_hi_ready"), sem("xT_ready")
        logits_made, part_ready, logits_ready = sem("logits_made"), sem("part_ready"), sem("logits_ready")
        route = sem("route")
        chosen_ready, chosen_exp = sem("chosen_ready"), sem("chosen_exp")
        a3_made, a1_made = sem("a3_made"), sem("a1_made")
        tanh_ready, gate_ready, hidden_ready = sem("tanh_ready"), sem("gate_ready"), sem("hidden_ready")
        h_hi_ready, h_ready = sem("h_hi_ready"), sem("h_ready")
        y_made, y_added = sem("y_made"), sem("y_added")
        piece_hi, piece_lo = sem("piece_hi"), sem("piece_lo")
        out_stored = sem("out_stored")
        LAST_PAIR = E // 2 - 1

        def routed(eng, step):
            def pair(i, last):
                for odd in range(2):
                    n = CHUNKS + 2 * CHUNKS * i + CHUNKS * odd
                    e = 2 * i + odd
                    step(n, 0, odd, e, 0, last)
                    with eng.Fori(0, 3) as j:
                        for k in range(2):
                            step(n + 2 * j + 1 + k, 2 * j + 1 + k, odd, e, 1 + k, last)

            with eng.Fori(0, LAST_PAIR) as i:
                pair(i, False)
            pair(LAST_PAIR, True)

        def tokens(c):
            if isinstance(c, int) and c == 0:
                return firstT_hi, firstT_lo, slice(0, CHUNK)
            return xT_hi, xT_lo, bass.ds((c - 1) * CHUNK, CHUNK)

        block = own.enter_context(nc.Block())

        @block.sync
        def _(sp):
            x1_rows = x1_dram.rearrange("(t p) d -> p t d", p=128)
            for c in [1, 0] + list(range(2, CHUNKS)):
                if c == CHUNKS - 1:
                    for i in range(2):
                        sp.wait_ge(x1_stored[i], 16 * (PAIRS + i))
                sp.dma_start(acc[:, c * TC:(c + 1) * TC, :], x1_rows[:, c * TC:(c + 1) * TC, :]).then_inc(x1_loaded[c], 16)
            def fetch(e, n):
                sp.wait_ge(piece_hi, PIECES * n)
                sp.wait_ge(piece_lo, PIECES * n)
                load_expert(sp, *(w[bass.ds(e, 1), :, :].rearrange("o d h -> (o d) h") for w in (W1, W3, W2)),
                            weights_in[2])

            with sp.Fori(1, E) as e:
                fetch(e, e)
            out_rows = outf.rearrange("(t p) d -> p t d", p=128)
            for c in range(CHUNKS):
                sp.wait_ge(y_added, TILES * E + TC * (c + 1))
                sp.dma_start(out_rows[:, c * TC:(c + 1) * TC, :], acc[:, c * TC:(c + 1) * TC, :]).then_inc(out_stored, 16)
            sp.wait_ge(out_stored, 16 * CHUNKS)

        @block.gpsimd
        def _(pool):
            pool.iota(iota[:], pattern=[[1, E]], base=0, channel_multiplier=0,
                      allow_small_or_imprecise_dtypes=True).then_inc(consts, 1)
            pool.memset(share[:, 0, :], 1.0).then_inc(consts, 1)

            def rstd_of(c):
                pool.wait_ge(var_ready, c)
                pool.tensor_scalar(var_eps[:], mean_var[:, :, 1], EPS, 1.0, ALU.add, ALU.mult).then_inc(var_eps_ready, 1)
                pool.wait_ge(var_eps_ready, c)
                pool.tensor_tensor(rstd[:], var_eps[:], minus_half[:], ALU.pow).then_inc(rstd_ready, 1)

            def lo_of_hidden(n, s):
                for m in range(MH):
                    pool.wait_ge(h_hi_ready, MH * n + m + 1)
                    pool.tensor_tensor(hT_lo[s][:, m, :], hidden[:, m % 2, :], hT_hi[s][:, m, :].bitcast(F32),
                                       ALU.subtract).then_inc(h_ready, 1)

            def lo_of_piece(n, j, buf):
                pool.wait_ge(piece_hi, PIECES * n + j + 1)
                cols = bass.ds(j * 512, 512)
                pool.tensor_tensor(w_lo[buf][:, cols], stage[:, cols], w_hi[buf][:, cols].bitcast(F32),
                                   ALU.subtract).then_inc(piece_lo, 1)

            rstd_of(1)
            for c in range(CHUNKS):
                lo_of_hidden(c, c % 2)
                if c + 2 < CHUNKS:
                    rstd_of(c + 2)
                if c > 0:
                    lo_of_piece(0, c - 1, 0)

            def step(n, c, buf, e, k, last):
                lo_of_hidden(n, (CHUNKS + CHUNKS * buf + k) % 2)
                if k > 0 and not (last and buf == 1):
                    lo_of_piece(e + 1, c - 1, 1 - buf)

            routed(pool, step)

        @block.scalar
        def _(act):
            def hi_of_x(c):
                hi, _, cols = tokens(c)
                for k in range(2):
                    act.wait_ge(xT_made, 2 * c + k - 1)
                    act.activation(hi[:, k, cols], X_BANK[k][:], ACT.Copy).then_inc(xT_hi_ready, 1)

            def chosen_exps():
                act.wait_ge(chosen_ready, 1)
                act.activation(chosen[:], chosen[:], ACT.Exp).then_inc(chosen_exp, 1)

            def units(n, s):
                for m in range(MH):
                    act.wait_ge(a3_made, MH * n + m + 1)
                    act.activation(tanh[:, m % 2, :], H_BANK[0][m % 2][:], ACT.Tanh, scale=0.5).then_inc(tanh_ready, 1)
                    act.wait_ge(hidden_ready, MH * n + m + 1)
                    act.activation(hT_hi[s][:, m, :], hidden[:, m % 2, :], ACT.Copy).then_inc(h_hi_ready, 1)
                    if isinstance(n, int) and n < CHUNKS - 1 and m == 2:
                        hi_of_x(n + 1)

            def hi_of_piece(n, j, buf):
                if not isinstance(j, int) or j == 0:
                    act.wait_ge(weights_in[2], 48 * (n + 1))
                cols = bass.ds(j * 512, 512)
                act.activation(w_hi[buf][:, cols], stage[:, cols], ACT.Copy).then_inc(piece_hi, 1)

            for c in range(CHUNKS):
                units(c, c % 2)
                if c + 1 == CHUNKS:
                    chosen_exps()
                if c > 0:
                    hi_of_piece(0, c - 1, 0)

            def step(n, c, buf, e, k, last):
                units(n, (CHUNKS + CHUNKS * buf + k) % 2)
                if k > 0 and not (last and buf == 1):
                    if k == 1:
                        act.wait_ge(y_made, TILES * (e + 1))
                    hi_of_piece(e + 1, c - 1, 1 - buf)

            routed(act, step)

        @block.vector
        def _(dve):
            def statistics(c):
                dve.wait_ge(x1_loaded[c], 16)
                for t in range(TC):
                    last = dve.bn_stats(stats[:, t, :], acc[:, c * TC + t, :])
                last.then_inc(stats_done, 1)
                dve.wait_ge(stats_done, c)
                for t in range(TC):
                    last = dve.bn_aggr(mean_var[:, t, :], stats[:, t, :])
                last.then_inc(var_ready, 1)

            def normed(c):
                dve.wait_ge(rstd_ready, c)
                wait(dve, xT_made, 2 * (c - 1))
                for t in range(TC):
                    last = dve.tensor_scalar(xn[:, t, :], acc[:, c * TC + t, :], mean_var[:, t, 0:1],
                                             rstd[:, t:t + 1], ALU.subtract, ALU.mult)
                last.then_inc(xn_ready, 1)

            def lo_of_x(c, k):
                hi, lo, cols = tokens(c)
                dve.wait_ge(xT_hi_ready, 2 * c + k - 1)
                dve.tensor_tensor(lo[:, k, cols], X_BANK[k][:], hi[:, k, cols].bitcast(F32),
                                  ALU.subtract).then_inc(xT_ready, 1)

            def link(count):
                dve.wait_ge(route, count)

            def take_logits(c):
                t = slice(c * TC, (c + 1) * TC)
                wait(dve, logits_made, c)
                src = (X_BANK[0] if c > 0 else first_logits)[:, 0:TC * 2 * E].rearrange("p (t e) -> p t e", e=2 * E)
                dve.tensor_scalar(part[:], src[:, :, E:], RSCALE, None, ALU.mult).then_inc(part_ready, 1)
                dve.wait_ge(part_ready, c + 1)
                dve.scalar_tensor_tensor(logits[:, t, :], src[:, :, 0:E], RSCALE, part[:],
                                         ALU.mult, ALU.add).then_inc(logits_ready, 1)
                dve.wait_ge(logits_ready, c + 1)
                dve.tensor_tensor(biased[:, t, :], logits[:, t, :],
                                  rb_sb[:].rearrange("p (o e) -> p o e", o=1).to_broadcast([128, TC, E]),
                                  ALU.add).then_inc(route, 1)

            def routing(c):
                link(3 * c + 1)
                for i in range(c * TC, (c + 1) * TC):
                    last = dve.max(top[:, i, :], biased[:, i, :])
                last.then_inc(route, 1)
                link(3 * c + 2)
                for i in range(c * TC, (c + 1) * TC):
                    last = dve.max_index(top_at[:, i, :], top[:, i, :], biased[:, i, :])
                last.then_inc(route, 1)

            def units(n, ms=range(MH)):
                for m in ms:
                    count = MH * n + m + 1
                    dve.wait_ge(tanh_ready, count)
                    wait(dve, hidden_ready, count - 1)
                    dve.scalar_tensor_tensor(gate[:], tanh[:, m % 2, :], 1.0, H_BANK[0][m % 2][:],
                                             ALU.add, ALU.mult).then_inc(gate_ready, 1)
                    dve.wait_ge(gate_ready, count)
                    dve.wait_ge(a1_made, count)
                    wait(dve, h_ready, count - 2)
                    dve.scalar_tensor_tensor(hidden[:, m % 2, :], gate[:], 0.5, H_BANK[1][m % 2][:],
                                             ALU.mult, ALU.mult).then_inc(hidden_ready, 1)

            def add_y(n, c, e, ts=range(TC)):
                for t in ts:
                    dve.wait_ge(y_made, TC * n + t + 1)
                    at = bass.ds(c * TC + t, 1)
                    dst = acc[:, at, :].rearrange("p o d -> p (o d)")
                    dve.scalar_tensor_tensor(dst, Y_BANK[t % 2][:, 0:D],
                                             share[:, bass.ds(e, 1), at].rearrange("p a b -> p (a b)"), dst,
                                             ALU.mult, ALU.add).then_inc(y_added, 1)

            def pick_two():
                n = 3 * CHUNKS
                link(n)
                dve.tensor_copy(top_atf[:], top_at[:, :, 0:2]).then_inc(route, 1)
                link(n + 1)
                all_e = iota[:].rearrange("p (o e) -> p o e", o=1).to_broadcast([128, TILES, E])
                for i in range(2):
                    last = dve.tensor_tensor(pick[:, i], all_e, top_atf[:, :, i:i + 1].to_broadcast([128, TILES, E]),
                                             ALU.is_equal)
                last.then_inc(route, 1)

            def their_logits():
                n = 3 * CHUNKS + 2
                link(n)
                for i in range(2):
                    last = dve.tensor_tensor(picked[:, i], pick[:, i], logits[:], ALU.mult)
                last.then_inc(route, 1)
                link(n + 1)
                for i in range(2):
                    last = dve.tensor_reduce(chosen[:, i, :], picked[:, i], AX.X, ALU.add)
                last.then_inc(route, 1)
                link(n + 2)
                dve.tensor_tensor(most[:], chosen[:, 0, :], chosen[:, 1, :], ALU.max).then_inc(route, 1)
                link(n + 3)
                for i in range(2):
                    last = dve.tensor_tensor(chosen[:, i, :], chosen[:, i, :], most[:], ALU.subtract)
                last.then_inc(chosen_ready, 1)

            def softmax_sum():
                n = 3 * CHUNKS + 5
                dve.wait_ge(chosen_exp, 1)
                dve.tensor_tensor(total[:], chosen[:, 0, :], chosen[:, 1, :], ALU.add).then_inc(route, 1)
                link(n + 1)
                dve.reciprocal(total_inv[:], total[:]).then_inc(route, 1)
                link(n + 2)
                for i in range(2):
                    last = dve.tensor_tensor(chosen[:, i, :], chosen[:, i, :], total_inv[:], ALU.mult)
                last.then_inc(route, 1)

            def shares():
                n = 3 * CHUNKS + 8
                link(n)
                for i in range(2):
                    last = dve.tensor_tensor(picked[:, i], pick[:, i],
                                             chosen[:, i, :].rearrange("p (t o) -> p t o", o=1).to_broadcast([128, TILES, E]),
                                             ALU.mult)
                last.then_inc(route, 1)
                link(n + 1)
                dve.tensor_tensor(share[:, 1:, :].rearrange("p e t -> p t e"), picked[:, 0], picked[:, 1],
                                  ALU.add).then_inc(route, 1)
                link(n + 2)

            statistics(1)
            for c in range(CHUNKS):
                more = c + 1 < CHUNKS
                take_logits(c)
                if c == 0:
                    dve.wait_ge(consts, 2)
                    dve.wait_ge(x1_loaded[0], 16)
                units(c, [0])
                if more:
                    normed(c + 1)
                    units(c, [1, 2])
                    for k in range(2):
                        lo_of_x(c + 1, k)
                else:
                    routing(c)
                    units(c, [1])
                    pick_two()
                    units(c, [2])
                    their_logits()
                units(c, [3])
                for t in range(TC):
                    if c > 0:
                        add_y(c - 1, c - 1, 0, [t])
                    if not more and t == 0:
                        softmax_sum()
                    if not more and t == 1:
                        shares()
                if more:
                    routing(c)
                if c + 2 < CHUNKS:
                    statistics(c + 2)

            def step(n, c, buf, e, k, last):
                units(n)
                if k == 0:
                    add_y(n - 1, CHUNKS - 1, e)
                else:
                    add_y(n - 1, c - 1, e + 1)

            routed(dve, step)
            add_y(CHUNKS * (E + 1) - 1, CHUNKS - 1, E)

        @block.tensor
        def _(pe):
            def product(o, pairs):
                for n, (lhsT, rhs) in enumerate(pairs):
                    mm = pe.matmul(o, lhsT, rhs, start=(n == 0), stop=(n == len(pairs) - 1))
                return mm

            def transposed(c):
                pe.wait_ge(xn_ready, c)
                wait(pe, xT_ready, 2 * (c - 1))
                wait(pe, logits_ready, c)
                for k in range(2):
                    for t in range(TC):
                        mm = pe.transpose(X_BANK[k][:, t * 128:(t + 1) * 128], xn[:, t, k * 128:(k + 1) * 128], ident[:])
                    mm.then_inc(xT_made, 1)

            def router(c):
                hi, lo, cols = tokens(c)
                for t in range(TC):
                    tok = slice(t * 128, (t + 1) * 128)
                    mm = product(X_BANK[0][:, t * 2 * E:(t + 1) * 2 * E],
                                 [(v[:, k, cols][:, tok], wr_split[:, k, :]) for k in range(2) for v in (hi, lo)])
                mm.then_inc(logits_made, 1)

            def up(n, c, buf):
                hi, lo, tok = tokens(c)
                for m in range(MH):
                    wait(pe, hidden_ready, MH * n + m - 1)
                    for o, base, made in ((H_BANK[0], 1024, a3_made), (H_BANK[1], 0, a1_made)):
                        cols = [slice(base + k * 512 + m * 128, base + k * 512 + m * 128 + 128) for k in range(2)]
                        product(o[m % 2][:], [(w[:, cols[k]], v[:, k, tok]) for k in range(2)
                                              for w, v in ((w_hi[buf], hi), (w_hi[buf], lo), (w_lo[buf], hi))]
                                ).then_inc(made, 1)
                    if isinstance(n, int) and n < CHUNKS - 1 and m == 2:
                        transposed(n + 1)

            def down(n, buf, s):
                pe.wait_ge(h_ready, MH * (n + 1))
                for t in range(TC):
                    wait(pe, y_added, TC * n + t - 1)
                    tok = slice(t * 128, (t + 1) * 128)
                    w2 = [slice(2048 + k * D, 2048 + (k + 1) * D) for k in range(MH)]
                    product(Y_BANK[t % 2][:, 0:D],
                            [(h[s][:, k, tok], w[buf][:, w2[k]]) for k in range(MH)
                             for h, w in ((hT_hi, w_hi), (hT_lo, w_hi), (hT_hi, w_lo))]).then_inc(y_made, 1)

            for c in range(CHUNKS):
                if c > 0:
                    pe.wait_ge(xT_ready, 2 * c)
                    router(c)
                up(c, c, 1)
                if c > 0:
                    down(c - 1, 1, (c - 1) % 2)

            def step(n, c, buf, e, k, last):
                if k == 0:
                    pe.wait_ge(piece_lo, PIECES * (e + 1))
                s = (CHUNKS + CHUNKS * buf + k) % 2
                up(n, c, buf)
                down(n - 1, 1 - buf if k == 0 else buf, 1 - s)

            routed(pe, step)
            down(CHUNKS * (E + 1) - 1, 1, (2 * CHUNKS + CHUNKS - 1) % 2)


_INS = ['x', 'ctx_768', 'L0_xattn_Wq', 'L0_xattn_Wk', 'L0_xattn_Wv', 'L0_xattn_Wout', 'L0_xattn_bout',
        'L0_ffn_Wr', 'L0_ffn_rb', 'L0_ffn_W1', 'L0_ffn_W2', 'L0_ffn_W3', 'L0_ffn_Ws1', 'L0_ffn_Ws2', 'L0_ffn_Ws3']


def kernel(**inputs):
    import numpy as _np
    import concourse.bacc as _bacc
    from concourse import mybir as _mybir
    from concourse.bass_utils import run_bass_kernel_spmd as _run

    nc = _bacc.Bacc("TRN2", target_bir_lowering=False, num_devices=1)
    arrays, args = {}, []
    for name in _INS:
        a = _np.ascontiguousarray(inputs[name])
        arrays[f"in_{name}"] = a
        args.append(nc.dram_tensor(f"in_{name}", a.shape, _mybir.dt.from_np(a.dtype), kind="ExternalInput").ap())
    out = nc.dram_tensor("out_0", inputs["x"].shape, _mybir.dt.float32, kind="ExternalOutput").ap()
    build(nc, *args, out)
    r = _run(nc, [arrays], core_ids=[0])
    return r.results[0]["out_0"]
```
